# Optimizing a Trainium2 kernel written in Bass

```python
import numpy as np
import jax
import jax.numpy as jnp

def _softmax(x, axis=-1):
    return jax.nn.softmax(x, axis=axis)

def _gelu(x):
    return jax.nn.gelu(x, approximate=True)

def _silu(x):
    return jax.nn.silu(x)

def _sigmoid(x):
    return jax.nn.sigmoid(x)

def _layernorm(x, axis=-1, eps=1e-05):
    m = jnp.mean(x, axis=axis, keepdims=True)
    v = jnp.var(x, axis=axis, keepdims=True)
    return (x - m) / jnp.sqrt(v + eps)

def _scatter_add(tgt, idx, src, axis=0):
    return tgt.at[idx].add(src)

def _segment_sum(src, seg, n):
    return jax.ops.segment_sum(src, seg, n)
kernel_name = 'mk_xattn_ffn_d2_seqx_r4_59702d'

def setup_inputs(seed: int=0):
    np.random.seed(seed)
    _w = jnp.asarray

    def _rec_inputs():
        import jax
        import jax.numpy as jnp
        _rk = jax.random.key(seed)
        x = -0.0002928 + 1 * jax.random.normal(jax.random.fold_in(_rk, 1), (16, 256, 256), jnp.float32)
        _lenS = 256 - jax.random.randint(jax.random.fold_in(_rk, 7), (16,), 0, max(1, 256 // 4) + 1, jnp.int32)
        _lenS2 = 77 - jax.random.randint(jax.random.fold_in(_rk, 8), (16,), 0, max(1, 77 // 4) + 1, jnp.int32)
        _ctx_1024P = jax.random.normal(jax.random.fold_in(_rk, 11), (16, 16, 256), jnp.float32)
        _ctx_1024c = jax.random.dirichlet(jax.random.fold_in(_rk, 511), 0.3 * jnp.ones((16,), jnp.float32), (16, 77))
        _ctx_1024t = jnp.einsum('bsk,bkd->bsd', _ctx_1024c, _ctx_1024P)
        _ctx_1024t = _ctx_1024t * jax.lax.rsqrt(jnp.mean(jnp.square(_ctx_1024t)) + 1e-12) * 0.953939
        ctx_1024 = -1.39393e-06 + 0.999914 * (_ctx_1024t + 0.3 * jax.random.normal(jax.random.fold_in(_rk, 611), (16, 77, 256), jnp.float32))
        return (x, ctx_1024)
    x, ctx_1024 = _rec_inputs()

    def _L0_xattn_setup():
        import jax, jax.numpy as jnp
        import numpy as np
        NUM_HEADS = 16
        D_MODEL = 256
        D_K = 64
        D_V = 64
        NEG_INF = -1000000000.0
        key = jax.random.key(seed)
        ks = jax.random.split(key, 7)
        B, S = (2, 512)
        Q = jax.random.normal(ks[0], (B, S, D_MODEL), dtype=jnp.float32)
        K = jax.random.normal(ks[1], (B, S, D_MODEL), dtype=jnp.float32)
        V = jax.random.normal(ks[2], (B, S, D_MODEL), dtype=jnp.float32)
        s = 1.0 / np.sqrt(D_MODEL)
        W_q = jax.random.normal(ks[3], (D_MODEL, D_K * NUM_HEADS), dtype=jnp.float32) * s
        W_k = jax.random.normal(ks[4], (D_MODEL, D_K), dtype=jnp.float32) * s
        W_v = jax.random.normal(ks[5], (D_MODEL, D_V), dtype=jnp.float32) * s
        W_o = jax.random.normal(ks[6], (D_V * NUM_HEADS, D_MODEL), dtype=jnp.float32) * (1.0 / np.sqrt(D_V * NUM_HEADS))
        return {'Q': Q, 'K': K, 'V': V, 'W_q': W_q, 'W_k': W_k, 'W_v': W_v, 'W_o': W_o}
    _L0_xattn_all = _L0_xattn_setup()
    _L0_xattn_in = {k: v for k, v in _L0_xattn_all.items() if k in ('W_q', 'W_k', 'W_v', 'W_o')}
    del _L0_xattn_all

    def _L0_ffn_setup():
        import jax, jax.numpy as jnp
        import numpy as np
        N_EMBD = 256
        N_STATE = 1024
        key = jax.random.key(seed)
        k_x, k_w1, k_b1, k_w2, k_b2 = jax.random.split(key, 5)
        x = jax.random.normal(k_x, (4, 512, N_EMBD), dtype=jnp.float32)
        w1 = jax.random.normal(k_w1, (N_EMBD, N_STATE), dtype=jnp.float32) * (1.0 / np.sqrt(N_EMBD))
        b1 = jax.random.normal(k_b1, (N_STATE,), dtype=jnp.float32) * 0.02
        w2 = jax.random.normal(k_w2, (N_STATE, N_EMBD), dtype=jnp.float32) * (1.0 / np.sqrt(N_STATE))
        b2 = jax.random.normal(k_b2, (N_EMBD,), dtype=jnp.float32) * 0.02
        return {'x': x, 'w1': w1, 'b1': b1, 'w2': w2, 'b2': b2}
    _L0_ffn_all = _L0_ffn_setup()
    _L0_ffn_in = {k: v for k, v in _L0_ffn_all.items() if k in ('w1', 'b1', 'w2', 'b2')}
    del _L0_ffn_all

    def _L1_xattn_setup():
        import jax, jax.numpy as jnp
        import numpy as np
        EMBED_DIM = 256
        NUM_HEADS = 16
        HEAD_DIM = EMBED_DIM // NUM_HEADS
        SCALE = HEAD_DIM ** (-0.5)
        key = jax.random.key(seed)
        k1, k2, k3, k4, k5, k6 = jax.random.split(key, 6)
        B, Tq, Tk = (2, 512, 512)
        std = EMBED_DIM ** (-0.5)
        return {'x_q': jax.random.normal(k1, (B, Tq, EMBED_DIM), jnp.float32), 'x_kv': jax.random.normal(k2, (B, Tk, EMBED_DIM), jnp.float32), 'w_q': jax.random.normal(k3, (EMBED_DIM, EMBED_DIM), jnp.float32) * std, 'w_kv': jax.random.normal(k4, (EMBED_DIM, 2 * EMBED_DIM), jnp.float32) * std, 'w_proj': jax.random.normal(k5, (EMBED_DIM, EMBED_DIM), jnp.float32) * std, 'w_rel': jax.random.normal(k6, (1, NUM_HEADS), jnp.float32) * 0.02}
    _L1_xattn_all = _L1_xattn_setup()
    _L1_xattn_in = {k: v for k, v in _L1_xattn_all.items() if k in ('w_q', 'w_kv', 'w_proj', 'w_rel')}
    del _L1_xattn_all

    def _L1_ffn_setup():
        import jax, jax.numpy as jnp
        import numpy as np
        LN_EPS = 1e-05
        NORM_EPS = 1e-12

        def _layernorm(x, gamma, beta):
            mu = x.mean(axis=-1, keepdims=True)
            var = ((x - mu) ** 2).mean(axis=-1, keepdims=True)
            return (x - mu) * jax.lax.rsqrt(var + LN_EPS) * gamma + beta

        def _l2norm(x, axis):
            n = jnp.sqrt((x ** 2).sum(axis=axis, keepdims=True))
            return x / jnp.maximum(n, NORM_EPS)
        key = jax.random.key(seed)
        ks = jax.random.split(key, 4)
        B, N, D, E, S, H = (64, 64, 256, 16, 16, 64)
        x = jax.random.normal(ks[0], (B, N, D), dtype=jnp.float32)
        mu = jax.random.normal(ks[1], (D, E, S), dtype=jnp.float32) / np.sqrt(D)
        w1 = jax.random.normal(ks[2], (E, D, H), dtype=jnp.float32) * np.sqrt(2.0 / D)
        w2 = jax.random.normal(ks[3], (E, H, D), dtype=jnp.float32) * np.sqrt(2.0 / (H + D))
        return {'x': x, 'ln_gamma': jnp.ones((D,), jnp.float32), 'ln_beta': jnp.zeros((D,), jnp.float32), 'mu': mu, 'scale': jnp.ones((1,), jnp.float32), 'w1': w1, 'b1': jnp.zeros((E, H), jnp.float32), 'w2': w2, 'b2': jnp.zeros((E, D), jnp.float32)}
    _L1_ffn_all = _L1_ffn_setup()
    _L1_ffn_in = {k: v for k, v in _L1_ffn_all.items() if k in ('ln_gamma', 'ln_beta', 'mu', 'scale', 'w1', 'b1', 'w2', 'b2')}
    del _L1_ffn_all
    return {'x': x, 'ctx_1024': ctx_1024, 'L0_xattn_W_q': _L0_xattn_in['W_q'], 'L0_xattn_W_k': _L0_xattn_in['W_k'], 'L0_xattn_W_v': _L0_xattn_in['W_v'], 'L0_xattn_W_o': _L0_xattn_in['W_o'], 'L0_ffn_w1': _L0_ffn_in['w1'], 'L0_ffn_b1': _L0_ffn_in['b1'], 'L0_ffn_w2': _L0_ffn_in['w2'], 'L0_ffn_b2': _L0_ffn_in['b2'], 'L1_xattn_w_q': _L1_xattn_in['w_q'], 'L1_xattn_w_kv': _L1_xattn_in['w_kv'], 'L1_xattn_w_proj': _L1_xattn_in['w_proj'], 'L1_xattn_w_rel': _L1_xattn_in['w_rel'], 'L1_ffn_ln_gamma': _L1_ffn_in['ln_gamma'], 'L1_ffn_ln_beta': _L1_ffn_in['ln_beta'], 'L1_ffn_mu': _L1_ffn_in['mu'], 'L1_ffn_scale': _L1_ffn_in['scale'], 'L1_ffn_w1': _L1_ffn_in['w1'], 'L1_ffn_b1': _L1_ffn_in['b1'], 'L1_ffn_w2': _L1_ffn_in['w2'], 'L1_ffn_b2': _L1_ffn_in['b2']}

def reference(x, ctx_1024, L0_xattn_W_q, L0_xattn_W_k, L0_xattn_W_v, L0_xattn_W_o, L0_ffn_w1, L0_ffn_b1, L0_ffn_w2, L0_ffn_b2, L1_xattn_w_q, L1_xattn_w_kv, L1_xattn_w_proj, L1_xattn_w_rel, L1_ffn_ln_gamma, L1_ffn_ln_beta, L1_ffn_mu, L1_ffn_scale, L1_ffn_w1, L1_ffn_b1, L1_ffn_w2, L1_ffn_b2):
    import jax
    import jax.numpy as jnp

    def _L0_xattn_ref(Q, K, V, W_q, W_k, W_v, W_o):
        import jax, jax.numpy as jnp
        import numpy as np
        NUM_HEADS = 16
        D_MODEL = 256
        D_K = 64
        D_V = 64
        NEG_INF = -1000000000.0
        B, Sq, _ = Q.shape
        Sk = K.shape[1]
        q = (Q @ W_q).reshape(B, Sq, NUM_HEADS, D_K).transpose(0, 2, 1, 3)
        k = K @ W_k
        v = V @ W_v
        scores = jnp.einsum('bhqd,bkd->bhqk', q, k) / jnp.sqrt(jnp.float32(D_K))
        causal = jnp.tril(jnp.ones((Sq, Sk), dtype=bool))
        scores = jnp.where(causal[None, None], scores, NEG_INF)
        attn = jax.nn.softmax(scores, axis=-1)
        out = jnp.einsum('bhqk,bkd->bhqd', attn, v)
        out = out.transpose(0, 2, 1, 3).reshape(B, Sq, NUM_HEADS * D_V)
        return out @ W_o

    def _L0_ffn_ref(x, w1, b1, w2, b2):
        import jax, jax.numpy as jnp
        import numpy as np
        N_EMBD = 256
        N_STATE = 1024
        h = jax.nn.gelu(jnp.einsum('bse,eh->bsh', x, w1) + b1, approximate=False)
        return jnp.einsum('bsh,he->bse', h, w2) + b2

    def _L1_xattn_ref(x_q, x_kv, w_q, w_kv, w_proj, w_rel):
        import jax, jax.numpy as jnp
        import numpy as np
        EMBED_DIM = 256
        NUM_HEADS = 16
        HEAD_DIM = EMBED_DIM // NUM_HEADS
        SCALE = HEAD_DIM ** (-0.5)
        B, Tq, _ = x_q.shape
        Tk = x_kv.shape[1]
        q = x_q @ w_q
        kv = x_kv @ w_kv
        k, v = jnp.split(kv, 2, axis=-1)

        def heads(y, T):
            return y.reshape(B, T, NUM_HEADS, HEAD_DIM).transpose(0, 2, 1, 3)
        q = heads(q, Tq)
        k = heads(k, Tk)
        v = heads(v, Tk)
        logits = jnp.einsum('bhqd,bhkd->bhqk', q, k) * SCALE
        rel = jnp.arange(Tq, dtype=jnp.float32)[:, None] - jnp.arange(Tk, dtype=jnp.float32)[None, :]
        bias = rel[..., None] * w_rel[0]
        bias = bias.transpose(2, 0, 1)[None]
        logits = logits + bias
        attn = jax.nn.softmax(logits, axis=-1)
        out = jnp.einsum('bhqk,bhkd->bhqd', attn, v)
        out = out.transpose(0, 2, 1, 3).reshape(B, Tq, EMBED_DIM)
        return out @ w_proj

    def _L1_ffn_ref(x, ln_gamma, ln_beta, mu, scale, w1, b1, w2, b2):
        import jax, jax.numpy as jnp
        import numpy as np
        LN_EPS = 1e-05
        NORM_EPS = 1e-12

        def _layernorm(x, gamma, beta):
            mu = x.mean(axis=-1, keepdims=True)
            var = ((x - mu) ** 2).mean(axis=-1, keepdims=True)
            return (x - mu) * jax.lax.rsqrt(var + LN_EPS) * gamma + beta

        def _l2norm(x, axis):
            n = jnp.sqrt((x ** 2).sum(axis=axis, keepdims=True))
            return x / jnp.maximum(n, NORM_EPS)
        B, N, D = x.shape
        _, E, S = mu.shape
        xn = _layernorm(x, ln_gamma, ln_beta)
        x_unit = _l2norm(xn, axis=-1)
        mu_unit = _l2norm(mu, axis=0)
        logits = jnp.einsum('bnd,des->bnes', x_unit * scale, mu_unit)
        dispatch = jax.nn.softmax(logits, axis=1)
        combine = jax.nn.softmax(logits.reshape(B, N, E * S), axis=-1).reshape(B, N, E, S)
        slot_in = jnp.einsum('bnd,bnes->besd', xn, dispatch)
        h = jax.nn.gelu(jnp.einsum('besd,edh->besh', slot_in, w1) + b1[None, :, None, :], approximate=False)
        slot_out = jnp.einsum('besh,ehd->besd', h, w2) + b2[None, :, None, :]
        out = jnp.einsum('besd,bnes->bnd', slot_out, combine)
        return out
    x = x + _L0_xattn_ref(_layernorm(x, axis=-1), ctx_1024, ctx_1024, L0_xattn_W_q, L0_xattn_W_k, L0_xattn_W_v, L0_xattn_W_o)
    x = x + _L0_ffn_ref(_layernorm(x, axis=-1), L0_ffn_w1, L0_ffn_b1, L0_ffn_w2, L0_ffn_b2)
    x = x + _L1_xattn_ref(_layernorm(x, axis=-1), ctx_1024, L1_xattn_w_q, L1_xattn_w_kv, L1_xattn_w_proj, L1_xattn_w_rel)
    x = x + _L1_ffn_ref(_layernorm(x, axis=-1), L1_ffn_ln_gamma, L1_ffn_ln_beta, L1_ffn_mu, L1_ffn_scale, L1_ffn_w1, L1_ffn_b1, L1_ffn_w2, L1_ffn_b2)
    return x

_drawn_inputs = setup_inputs


def setup_inputs(seed=0):
    import zlib

    import numpy as np

    out = dict(_drawn_inputs(seed))
    spreads = {'L1_ffn_ln_gamma': (1.0, 0.6),
     'L1_ffn_ln_beta': (0.0, 0.8),
     'L1_ffn_b1': (0.0, 0.8),
     'L1_ffn_b2': (0.0, 0.498)}
    factors = {'L0_ffn_b1': 6.045, 'L0_ffn_b2': 4.092, 'L1_ffn_mu': 8.0}
    for name, (base, spread) in spreads.items():
        noise = np.random.default_rng([zlib.crc32(name.encode()), seed]).standard_normal(out[name].shape)
        drawn = base * np.exp(spread * noise) if base else spread * noise
        out[name] = jnp.asarray(drawn.astype(out[name].dtype))
    for name, factor in factors.items():
        out[name] = (out[name] * factor).astype(out[name].dtype)
    return out
```

```python
from contextlib import ExitStack

import numpy as np
import concourse.bass as bass
from concourse import mybir

ALU = mybir.AluOpType
ACT = mybir.ActivationFunctionType
AX = mybir.AxisListType.X
F32 = mybir.dt.float32
F32R = mybir.dt.float32r
BF16 = mybir.dt.bfloat16

P = 128
B = 16
N = 256
NC = N // P
D = 256
DC = D // P
SK = 77
H = 16
HP = H // 2
PAIR = 2 * SK
DK0 = 64
DK1 = 16
FF = 1024
FC = FF // P
E = 16
S = 16
HID = 64
LN_EPS = 1e-5
PASSES = ((0, 0), (0, 1), (1, 0))


def at_least(eng, sem, value):
    if not isinstance(value, int) or value > 0:
        eng.wait_ge(sem, value)


def wait_apart(eng, sem, value):
    at_least(eng.engine, sem, value)
    if not isinstance(value, int):
        eng.engine.sem_inc(eng.ticks, 1)


class Ticking:

    def __init__(self, engine, ticks):
        self.engine, self.ticks = engine, ticks


def fp32_of(ap):
    return ap.bitcast(F32)


class Memory:

    def __init__(self, nc, stack, prefix):
        self.nc, self.stack, self.prefix, self.sems = nc, stack, prefix, []

    def sb(self, name, shape, dt=F32):
        return self.stack.enter_context(self.nc.sbuf_tensor(f"{self.prefix}_{name}", shape, dt))

    def ps(self, name, cols=512, dt=F32):
        return self.stack.enter_context(self.nc.psum_tensor(f"{self.prefix}_{name}", [P, cols], dt))

    def sem(self, name):
        self.sems.append(self.nc.alloc_semaphore(f"{self.prefix}_{name}"))
        return self.sems[-1]

    def end_phase(self):
        self.nc.clear_and_free_semaphores(self.sems)
        self.nc.all_engine_barrier()

    def split(self, name, shape):
        return self.sb(name + "_hi", shape, F32R), self.sb(name + "_lo", shape, F32R)


def prologue(nc, d, st):
    G = 4
    GK = G * SK
    VC = DK0 + D
    with ExitStack() as stack:
        m = Memory(nc, stack, "pro")
        w_raw = m.sb("w_raw", [P, DC, 2 * DK0 + 2 * D])
        wk = m.split("wk", [P, DC, P + D])
        wv = m.split("wv", [P, DC, VC])
        ctx_in = m.sb("ctx_in", [SK, G, D])
        ctxT = m.split("ctxT", [P, DC, GK])
        ctxT_ps = [m.ps(f"ctxT_ps{c}") for c in range(DC)]
        key_ps = [m.ps(f"key_ps{j}") for j in range(3)]
        val_ps = [m.ps(f"val_ps{j}") for j in range(2)]
        x_in = m.sem("x_in")
        half_ready = m.sem("half_ready")
        const_in = m.sem("const_in")
        w_in = m.sem("w_in")
        ctx_read = m.sem("ctx_read")
        wk_ready, wv_ready, whi = m.sem("wk_ready"), m.sem("wv_ready"), m.sem("whi")
        ctxT_psum, ctxT_hi, ctxT_lo = m.sem("ctxT_psum"), m.sem("ctxT_hi"), m.sem("ctxT_lo")
        key_psum, key_done = m.sem("key_psum"), m.sem("key_done")
        val_psum, val_done = m.sem("val_psum"), m.sem("val_done")
        stack.callback(m.end_phase)
        block = stack.enter_context(nc.Block())

        @block.sync
        def _(sp):
            sp.dma_start(st.ident[:, :], d["ident"]).then_inc(const_in, 16)
            sp.dma_start(ctx_in[:, :, :], d["ctx"][0:G].rearrange("b k e -> k b e")).then_inc(ctx_read, 16)
            sp.dma_start(w_raw[:, :, 0:DK0], d["L0_xattn_W_k"].rearrange("(c p) n -> p c n", p=P)).then_inc(w_in, 16)
            sp.dma_start(w_raw[:, :, DK0:2 * DK0], d["L0_xattn_W_v"].rearrange("(c p) n -> p c n", p=P)).then_inc(w_in, 16)
            sp.dma_start(w_raw[:, :, 2 * DK0:], d["L1_xattn_w_kv"].rearrange("(c p) n -> p c n", p=P)).then_inc(w_in, 16)
            sp.dma_start(st.head_mask0[:, :], d["head_mask0"]).then_inc(const_in, 16)
            sp.dma_start(st.head_mask1[:, :], d["head_mask1"]).then_inc(const_in, 16)
            for b in range(B):
                sp.dma_start(st.x[:, b, :, :], d["x"][b].rearrange("(q p) e -> p q e", p=P)).then_inc(x_in, 16)
            with sp.Fori(1, B // G) as g:
                sp.wait_ge(ctxT_psum, g * DC)
                sp.dma_start(ctx_in[:, :, :], d["ctx"][bass.ds(g * G, G)].rearrange("b k e -> k b e")).then_inc(ctx_read, 16)
            sp.wait_ge(x_in, 16 * B)
            sp.wait_ge(const_in, 48)

        @block.gpsimd
        def _(pool):
            poolt = Ticking(pool, m.sem("pool_ticks"))
            pool.memset(st.minus_half[:, :], -0.5).then_inc(half_ready, 1)
            wait_apart(poolt, half_ready, 1)

        @block.tensor
        def _(pe):
            pe.wait_ge(const_in, 48)

            def group(g):
                pe.wait_ge(ctx_read, g * 16 + 16)
                for c in range(DC):
                    at_least(pe, ctxT_lo, g * DC + c - DC + 1)
                    for b in range(G):
                        last = nc.tensor.transpose(ctxT_ps[c][:, b * SK:(b + 1) * SK],
                                                   ctx_in[0:SK, b, c * P:(c + 1) * P], st.ident[0:SK, 0:SK])
                    last.then_inc(ctxT_psum, 1)
                pe.wait_ge(ctxT_lo, g * DC + DC)
                for j in range(3):
                    if j == 0:
                        pe.wait_ge(wk_ready, 1)
                    at_least(pe, key_done, g * 3 + j - 2)
                    for n, (c, (a, b)) in enumerate((c, ab) for c in range(DC) for ab in PASSES):
                        last = nc.tensor.matmul(key_ps[j][:, 0:GK], wk[a][:, c, j * P:(j + 1) * P],
                                                ctxT[b][:, c, :], start=n == 0, stop=n == 5)
                    last.then_inc(key_psum, 1)
                for k in range(G):
                    if k == 0:
                        pe.wait_ge(wv_ready, 1)
                    at_least(pe, val_done, g * G + k - 1)
                    for n, (c, (a, b)) in enumerate((c, ab) for c in range(DC) for ab in PASSES):
                        last = nc.tensor.matmul(val_ps[k % 2][0:SK, 0:VC], ctxT[a][:, c, k * SK:(k + 1) * SK],
                                                wv[b][:, c, :], start=n == 0, stop=n == 5)
                    last.then_inc(val_psum, 1)

            group(0)
            with pe.Fori(1, B // G) as g:
                group(g)

        @block.scalar
        def _(act):
            act.wait_ge(w_in, 48)
            for t, (out, lo, hi) in enumerate(((wk[0][:, :, 0:DK0], 0, DK0), (wk[0][:, :, DK0:P], 0, DK0),
                                               (wk[0][:, :, P:], 2 * DK0, 2 * DK0 + D),
                                               (wv[0][:, :, 0:DK0], DK0, 2 * DK0),
                                               (wv[0][:, :, DK0:], 2 * DK0 + D, 2 * DK0 + 2 * D))):
                nc.scalar.copy(out, w_raw[:, :, lo:hi]).then_inc(whi, 1)

            def group(g):
                for c in range(DC):
                    act.wait_ge(ctxT_psum, g * DC + c + 1)
                    at_least(act, val_psum, g * G)
                    nc.scalar.copy(ctxT[0][:, c, :], ctxT_ps[c][:, 0:GK]).then_inc(ctxT_hi, 1)
                for k in range(G):
                    act.wait_ge(val_psum, g * G + k + 1)
                    nc.scalar.copy(st.val0[0:SK, bass.ds(g * G + k, 1), :], val_ps[k % 2][0:SK, 0:DK0].unsqueeze(1))
                    nc.scalar.copy(st.val1[0:SK, bass.ds(g * G + k, 1), :],
                                   val_ps[k % 2][0:SK, DK0:VC].unsqueeze(1)).then_inc(val_done, 1)

            group(0)
            with act.Fori(1, B // G) as g:
                group(g)

        @block.vector
        def _(dve):
            for t, (i, a, b, lo, hi) in enumerate(((wk, 0, DK0, 0, DK0), (wk, DK0, P, 0, DK0),
                                                   (wk, P, P + D, 2 * DK0, 2 * DK0 + D),
                                                   (wv, 0, DK0, DK0, 2 * DK0),
                                                   (wv, DK0, VC, 2 * DK0 + D, 2 * DK0 + 2 * D))):
                dve.wait_ge(whi, t + 1)
                op = nc.vector.tensor_tensor(i[1][:, :, a:b], w_raw[:, :, lo:hi], fp32_of(i[0][:, :, a:b]), ALU.subtract)
                if t == 2:
                    op.then_inc(wk_ready, 1)
                if t == 4:
                    op.then_inc(wv_ready, 1)

            def group(g):
                for c in range(DC):
                    dve.wait_ge(ctxT_hi, g * DC + c + 1)
                    at_least(dve, val_psum, g * G)
                    nc.vector.tensor_tensor(ctxT[1][:, c, :], ctxT_ps[c][:, 0:GK], fp32_of(ctxT[0][:, c, :]),
                                            ALU.subtract).then_inc(ctxT_lo, 1)
                for j in range(3):
                    dve.wait_ge(key_psum, g * 3 + j + 1)
                    keys = key_ps[j][:, 0:GK].rearrange("p (b k) -> p b k", b=G)
                    out = st.key0[:, bass.ds(g * G, G), :] if j == 0 else st.key1[:, j - 1, bass.ds(g * G, G), :]
                    nc.vector.tensor_copy(out, keys).then_inc(key_done, 1)

            group(0)
            with dve.Fori(1, B // G) as g:
                group(g)


def x_rows(st, b, q):
    return st.x[:, bass.ds(b, 1), q, :].rearrange("p b e -> p (b e)")


class LayerNorm:

    def __init__(self, nc, m, st):
        self.nc, self.st = nc, st
        self.xn = m.sb("xn", [P, NC, D])
        self.stats = m.sb("stats", [P, NC, 6])
        self.mean_var = m.sb("mean_var", [P, NC, 2])
        self.var_eps = m.sb("var_eps", [P, NC])
        self.rstd = m.sb("rstd", [P, NC])
        self.ticks = m.sem("ln_pool_ticks"), m.sem("ln_dve_ticks")
        self.stats_step, self.stats_ready = m.sem("stats_step"), m.sem("stats_ready")
        self.var_ready, self.rstd_ready, self.ready = m.sem("var_ready"), m.sem("rstd_ready"), m.sem("ln_ready")

    def statistics(self, dve, f):
        at_least(dve, self.ready, NC * f)
        for q in range(NC):
            self.nc.vector.bn_stats(self.stats[:, q, :], x_rows(self.st, f, q)).then_inc(self.stats_step, 1)
        for q in range(NC):
            wait_apart(Ticking(dve, self.ticks[1]), self.stats_step, NC * f + q + 1)
            self.nc.vector.bn_aggr(self.mean_var[:, q, :], self.stats[:, q, :]).then_inc(self.stats_ready, 1)

    def inverse_deviation(self, pool, f):
        poolt = Ticking(pool, self.ticks[0])
        wait_apart(poolt, self.stats_ready, NC * f + NC)
        wait_apart(poolt, self.ready, NC * f)
        self.nc.gpsimd.tensor_scalar(self.var_eps[:, :], self.mean_var[:, :, 1], LN_EPS, None,
                                     ALU.add).then_inc(self.var_ready, 1)
        wait_apart(poolt, self.var_ready, f + 1)
        self.nc.gpsimd.tensor_tensor(self.rstd[:, :], self.var_eps[:, :], self.st.minus_half[:, 0:NC],
                                     ALU.pow).then_inc(self.rstd_ready, 1)

    def normalise(self, dve, f, read, reads):
        dve.wait_ge(self.rstd_ready, f + 1)
        at_least(dve, read, reads * f)
        for q in range(NC):
            self.nc.vector.tensor_scalar(self.xn[:, q, :], x_rows(self.st, f, q), self.mean_var[:, q, 0:1],
                                         self.rstd[:, q:q + 1], ALU.subtract, ALU.mult).then_inc(self.ready, 1)


def attention(nc, d, st, index):
    with ExitStack() as stack:
        m = Memory(nc, stack, f"att{index}")
        L0 = index == 0
        dk = DK0 if L0 else DK1
        QW = H * dk
        CH = QW // P
        PC = HP // CH
        HC = 2 * PC
        scale = dk ** -0.5
        w_raw = m.sb("w_raw", [P, 2048])
        wq = m.split("wq", [P, DC, QW])
        wo = m.split("wo", [P, CH, D])
        key, val = (st.key0, st.val0) if L0 else (st.key1, st.val1)
        head_mask = st.head_mask0 if L0 else st.head_mask1
        step_of_query = {c - 1: c for c in range(1, CH)}
        RING = 4
        KC = 1 if L0 else CH
        KH = 2 if L0 else HC

        ln = LayerNorm(nc, m, st)
        xT = m.split("xT", [P, DC, N])
        qT = [m.sb(f"qT{i}", [P, N]) for i in range(2)]
        keys = m.sb("keys", [P, KC, KH, SK])
        vals = m.split("vals", [P, (2 if L0 else H) * P + HC * dk])
        mx = [m.sb(f"mx{i}", [P, 2 * NC]) for i in range(2)]
        ex = [m.sb(f"ex{i}", [P, 2 * NC, SK]) for i in range(RING)]
        rsum = [m.sb(f"rsum{i}", [P, 2 * NC]) for i in range(RING)]
        rinv = [m.sb(f"rinv{i}", [P, 2 * NC]) for i in range(RING)]
        PW = (H - 1) * SK + P
        prob = m.sb("prob", [P, NC, PW])
        pT = [m.split(f"pT{i}", [P, 2 * N]) for i in range(2)]
        oT = m.split("oT", [P, CH, N])
        if L0:
            ident16 = m.sb("ident16", [P, P], BF16)
            causal_raw = m.sb("causal_raw", [P, PAIR])
            causal16 = m.sb("causal16", [P, PAIR], BF16)
        else:
            pos_raw = m.sb("pos_raw", [P, 2, N])
            pos16 = m.sb("pos16", [P, 2, N], BF16)
            slope = m.sb("slope", [P, 2, H, SK])
            neg_k = m.sb("neg_k", [P, SK])
            w_rel = m.sb("w_rel", [P, H])
            part = m.sb("part", [P, 2, H, SK])
            part16 = m.sb("part16", [P, 2, H, SK], BF16)
            bias16 = m.sb("bias16", [P, 2, H, SK], BF16)

        q_bank = [m.ps(f"q_bank{i}") for i in range(2)]
        s_bank = [m.ps(f"s_bank{i}") for i in range(2)]
        t_bank = [m.ps(f"t_bank{i}") for i in range(2)]
        o_bank = [m.ps(f"o_bank{i}") for i in range(2)]

        w_in, w_hi, w_ready = m.sem("w_in"), m.sem("w_hi"), m.sem("w_ready")
        wo_in = m.sem("wo_in")
        c_in, c_ready, zeroed, c_step = m.sem("c_in"), m.sem("c_ready"), m.sem("zeroed"), m.sem("c_step")
        xt_psum, xt_hi, xt_lo = m.sem("xt_psum"), m.sem("xt_hi"), m.sem("xt_lo")
        q_psum, q_ready = m.sem("q_psum"), m.sem("q_ready")
        keys_ready, vals_hi, vals_ready = m.sem("keys_ready"), m.sem("vals_hi"), m.sem("vals_ready")
        s_psum, mx_ready, shifted, ex_ready = m.sem("s_psum"), m.sem("mx_ready"), m.sem("shifted"), m.sem("ex_ready")
        sum_ready, inv_ready, p_ready = m.sem("sum_ready"), m.sem("inv_ready"), m.sem("p_ready")
        t_psum, pt_hi, pt_lo = m.sem("t_psum"), m.sem("pt_hi"), m.sem("pt_lo")
        pv_done, ot_hi, ot_lo = m.sem("pv_done"), m.sem("ot_hi"), m.sem("ot_lo")
        proj_psum, x_done = m.sem("proj_psum"), m.sem("x_done")
        stack.callback(m.end_phase)
        block = stack.enter_context(nc.Block())

        def loop(eng, body):
            body(0, True, False, True)
            body(1, True, True, True)
            with eng.Fori(2, B - 1) as f:
                body(f, True, True, True)
            body(B - 1, True, True, False)
            body(B, False, True, False)

        W_IN = 6

        @block.sync
        def _(sp):
            pre = f"L{index}_xattn_"
            names = ("W_q", "W_o") if L0 else ("w_q", "w_proj")
            sp.dma_start(w_raw[:, 0:DC * QW].rearrange("p (c n) -> p c n", c=DC),
                         d[pre + names[0]].rearrange("(c p) n -> p c n", p=P)).then_inc(w_in, 16)
            if L0:
                sp.dma_start(causal_raw[:, :], d["causal"]).then_inc(c_in, 16)
            else:
                sp.wait_ge(zeroed, 4)
                sp.dma_start(pos_raw[:, :, :], d["positions"]).then_inc(c_in, 16)
                sp.dma_start(neg_k[:, :], d["neg_k"]).then_inc(c_in, 16)
                for row in (0, 32, 64):
                    sp.dma_start(w_rel[row:row + 1, :], d["L1_xattn_w_rel"]).then_inc(c_in, 16)
            sp.wait_ge(w_ready, 1)
            sp.dma_start(w_raw[:, 0:CH * D].rearrange("p (c n) -> p c n", c=CH),
                         d[pre + names[1]].rearrange("(c p) n -> p c n", p=P)).then_inc(wo_in, 16)

        @block.tensor
        def _(pe):
            def transpose_x(f):
                for c in range(DC):
                    pe.wait_ge(ln.ready, NC * f + NC)
                    if not isinstance(f, int) or f > 0:
                        pe.wait_ge(q_ready, CH * f - DC + c + 1)
                    for q in range(NC):
                        last = nc.tensor.transpose(q_bank[c][:, q * P:(q + 1) * P],
                                                   ln.xn[:, q, c * P:(c + 1) * P], st.ident[:, :])
                    last.then_inc(xt_psum, 1)

            def queries(f, c):
                pe.wait_ge(xt_lo, DC * f + DC)
                if c >= 2:
                    pe.wait_ge(q_ready, CH * f + c - 1)
                for n, (k, (a, b)) in enumerate((k, ab) for k in range(DC) for ab in PASSES):
                    last = nc.tensor.matmul(q_bank[c % 2][:, 0:N], wq[a][:, k, c * P:(c + 1) * P],
                                            xT[b][:, k, :], start=n == 0, stop=n == 5)
                last.then_inc(q_psum, 1)

            def scores(f, t):
                c = t // PC
                pe.wait_ge(q_ready, CH * f + c + 1)
                if t % (HP // KC) == 0:
                    pe.wait_ge(keys_ready, KC * f + t * KC // HP + 1)
                at_least(pe, shifted, HP * f + t - 1)
                if t == 0:
                    at_least(pe, x_done, NC * (f - 2) + 1)
                kc, h0 = (0, 0) if L0 else (c, 2 * (t % PC))
                for q in range(NC):
                    out = s_bank[t % 2][:, q * PAIR:(q + 1) * PAIR]
                    first = True
                    if L0 and q == 0:
                        nc.tensor.matmul(out, ident16[:, :], causal16[:, :], start=True, stop=False)
                        first = False
                    if not L0:
                        for r in range(2):
                            nc.tensor.matmul(out, pos16[:, r, q * P:(q + 1) * P],
                                             bias16[:, r, 2 * t:2 * t + 2, :], start=r == 0, stop=False)
                        first = False
                    last = nc.tensor.matmul(out, qT[c % 2][:, q * P:(q + 1) * P], keys[:, kc, h0:h0 + 2, :],
                                            start=first, stop=True)
                last.then_inc(s_psum, 1)

            def transpose_p(g, t):
                pe.wait_ge(p_ready, HP * g + min(t + 2, HP))
                at_least(pe, pt_lo, HP * g + t - 1)
                for h in range(2):
                    for q in range(NC):
                        last = nc.tensor.transpose(t_bank[t % 2][:, h * N + q * P:h * N + (q + 1) * P],
                                                   prob[:, q, (2 * t + h) * SK:(2 * t + h) * SK + P], st.ident[:, :])
                last.then_inc(t_psum, 1)

            def weigh_values(g, t):
                j = t // PC
                pe.wait_ge(pt_lo, HP * g + t + 1)
                if t % (HP // KC) == 0:
                    pe.wait_ge(vals_ready, KC * g + t * KC // HP + 1)
                if t % PC == 0:
                    if j == 0:
                        at_least(pe, x_done, NC * g)
                    else:
                        at_least(pe, ot_lo, CH * g + max(j - 1, 0))
                for h in range(2):
                    v = h if L0 else 2 * t + h
                    for n, (a, b) in enumerate(PASSES):
                        last = nc.tensor.matmul(o_bank[j % 2][:, 0:N], vals[a][:, v * P:(v + 1) * P], pT[t % 2][b][:, h * N:(h + 1) * N],
                                                start=t % PC == 0 and h == 0 and n == 0,
                                                stop=t % PC == PC - 1 and h == 1 and n == 2)
                last.then_inc(pv_done, 1)

            def project(g, q, chunks):
                for j in chunks:
                    pe.wait_ge(ot_lo, CH * g + j + 1)
                    for n, (a, b) in enumerate(PASSES):
                        last = nc.tensor.matmul((s_bank[0], o_bank[0])[q][:, 0:D], oT[a][:, j, q * P:(q + 1) * P],
                                                wo[b][:, j, :], start=j == 0 and n == 0, stop=j == CH - 1 and n == 2)
                if j == CH - 1:
                    last.then_inc(proj_psum, 1)

            def batch(f, front, back, following):
                g = f - 1
                for t in range(HP):
                    if front and t in step_of_query:
                        queries(f, step_of_query[t])
                    if back:
                        transpose_p(g, t)
                    if front:
                        scores(f, t)
                    if back and t >= 1:
                        weigh_values(g, t - 1)
                if following:
                    transpose_x(f + 1)
                if back:
                    pe.wait_ge(shifted, HP * f + HP - 1 if front else HP * B)
                    if CH > 2:
                        project(g, 0, range(CH - 2))
                    weigh_values(g, HP - 1)
                    project(g, 0, range(max(CH - 2, 0), CH - 1))
                    project(g, 1, range(CH - 1))
                if following:
                    queries(f + 1, 0)
                if back:
                    for q in range(NC):
                        project(g, q, (CH - 1,))

            pe.wait_ge(c_ready, 1)
            transpose_x(0)
            pe.wait_ge(w_ready, 1)
            queries(0, 0)
            pe.wait_ge(w_ready, 2)
            loop(pe, batch)

        @block.scalar
        def _(act):
            for i, (w, rows) in enumerate(((wq, DC), (wo, CH))):
                act.wait_ge(w_in if i == 0 else wo_in, 16)
                raw = w_raw[:, 0:DC * QW].rearrange("p (c n) -> p c n", c=rows)
                nc.scalar.copy(w[0][:, :, :], raw).then_inc(w_hi, 1)

            def transposed_x(f):
                for c in range(DC):
                    act.wait_ge(xt_psum, DC * f + c + 1)
                    nc.scalar.copy(xT[0][:, c, :], q_bank[c][:, 0:N]).then_inc(xt_hi, 1)

            def batch(f, front, back, following):
                g = f - 1
                for t in range(HP + 1):
                    if front and t in step_of_query:
                        scale_queries(f, step_of_query[t])
                    if back and t < HP:
                        act.wait_ge(t_psum, HP * g + t + 1)
                        at_least(act, pv_done, HP * g + t - 1)
                        nc.scalar.copy(pT[t % 2][0][:, :], t_bank[t % 2][:, :]).then_inc(pt_hi, 1)
                    if front and t >= 1:
                        act.wait_ge(shifted, HP * f + t)
                        e = ex[(t - 1) % RING]
                        nc.scalar.activation(e[:, :, :], e[:, :, :], ACT.Exp).then_inc(ex_ready, 1)
                    if back and t >= 2 and (t - 1) % PC == 0:
                        copy_heads(g, (t - 1) // PC - 1)
                if following:
                    transposed_x(f + 1)
                if back:
                    copy_heads(g, CH - 1)
                if following:
                    scale_queries(f + 1, 0)

            def scale_queries(f, c):
                act.wait_ge(q_psum, CH * f + c + 1)
                at_least(act, s_psum, HP * f + (c - 1) * PC)
                nc.scalar.mul(qT[c % 2][:, :], q_bank[c % 2][:, 0:N], scale).then_inc(q_ready, 1)

            def copy_heads(g, j):
                act.wait_ge(pv_done, HP * g + (j + 1) * PC)
                at_least(act, proj_psum, NC * g)
                nc.scalar.copy(oT[0][:, j, :], o_bank[j % 2][:, 0:N]).then_inc(ot_hi, 1)

            transposed_x(0)
            scale_queries(0, 0)
            loop(act, batch)

        @block.vector
        def _(dve):
            def transposed_x(f):
                for c in range(DC):
                    dve.wait_ge(xt_hi, DC * f + c + 1)
                    nc.vector.tensor_tensor(xT[1][:, c, :], q_bank[c][:, 0:N], fp32_of(xT[0][:, c, :]),
                                            ALU.subtract).then_inc(xt_lo, 1)

            def row_scores(t):
                return s_bank[t % 2][:, 0:NC * PAIR].rearrange("p (r k) -> p r k", k=SK)

            def find_maxima(f, t):
                dve.wait_ge(s_psum, HP * f + t + 1)
                at_least(dve, shifted, HP * f + t - 1)
                nc.vector.tensor_reduce(mx[t % 2][:, :], row_scores(t), AX, ALU.max).then_inc(mx_ready, 1)

            def shift(f, t):
                dve.wait_ge(mx_ready, HP * f + t + 1)
                at_least(dve, p_ready, HP * f + t - RING + 1)
                nc.vector.tensor_tensor(ex[t % RING][:, :, :], row_scores(t),
                                        mx[t % 2][:, :].unsqueeze(2).to_broadcast([P, 2 * NC, SK]),
                                        ALU.subtract).then_inc(shifted, 1)

            def add_up(f, t):
                dve.wait_ge(ex_ready, HP * f + t + 1)
                nc.vector.tensor_reduce(rsum[t % RING][:, :], ex[t % RING][:, :, :], AX, ALU.add).then_inc(sum_ready, 1)

            def invert(f, t):
                dve.wait_ge(sum_ready, HP * f + t + 1)
                at_least(dve, p_ready, HP * f + t - RING + 1)
                nc.vector.reciprocal(rinv[t % RING][:, :], rsum[t % RING][:, :]).then_inc(inv_ready, 1)

            def split_heads(g, j):
                dve.wait_ge(ot_hi, CH * g + j + 1)
                nc.vector.tensor_tensor(oT[1][:, j, :], o_bank[j % 2][:, 0:N], fp32_of(oT[0][:, j, :]),
                                        ALU.subtract).then_inc(ot_lo, 1)

            def batch(f, front, back, following):
                g = f - 1
                for t in range(HP + 2):
                    if front and 1 <= t <= HP:
                        find_maxima(f, t - 1)
                    if front and t >= 2:
                        add_up(f, t - 2)
                    if front and 1 <= t <= HP:
                        shift(f, t - 1)
                    if front and t >= 2:
                        invert(f, t - 2)
                    if back and t < HP:
                        dve.wait_ge(pt_hi, HP * g + t + 1)
                        nc.vector.tensor_tensor(pT[t % 2][1][:, :], t_bank[t % 2][:, :], fp32_of(pT[t % 2][0][:, :]),
                                                ALU.subtract).then_inc(pt_lo, 1)
                    if back and 2 <= t <= HP and (t - 1) % PC == 0:
                        split_heads(g, (t - 1) // PC - 1)
                    if following and t == HP // 2:
                        ln.statistics(dve, f + 1)
                    if following and t == HP // 2 + 2:
                        ln.normalise(dve, f + 1, xt_psum, DC)
                    if following and t == HP:
                        transposed_x(f + 1)
                if back:
                    split_heads(g, CH - 1)
                    for q in range(NC):
                        dve.wait_ge(proj_psum, NC * g + q + 1)
                        nc.vector.tensor_tensor(x_rows(st, g, q), (s_bank[0], o_bank[0])[q][:, 0:D], x_rows(st, g, q), ALU.add).then_inc(x_done, 1)

            if L0:
                dve.wait_ge(c_in, 16)
                nc.vector.tensor_copy(ident16[:, :], st.ident[:, :])
                nc.vector.tensor_copy(causal16[:, :], causal_raw[:, :]).then_inc(c_ready, 1)
            else:
                dve.wait_ge(c_in, 16 * 5)
                nc.vector.tensor_copy(pos16[:, :, :], pos_raw[:, :, :])
                nc.vector.tensor_copy(slope[:, 0, :, :], w_rel[:, :].unsqueeze(2).to_broadcast([P, H, SK]))
                nc.vector.tensor_tensor(slope[:, 1, :, :], w_rel[:, :].unsqueeze(2).to_broadcast([P, H, SK]),
                                        neg_k[:, :].unsqueeze(1).to_broadcast([P, H, SK]), ALU.mult).then_inc(c_step, 1)
                n = 1
                for i, row in enumerate((0, 32, 64)):
                    dve.wait_ge(c_step, n)
                    nc.vector.tensor_copy(part16[:, :, :, :], slope[:, :, :, :]).then_inc(c_step, 1)
                    dve.wait_ge(c_step, n + 1)
                    last = nc.vector.tensor_copy(bias16[row:row + 1, :, :, :], part16[row:row + 1, :, :, :])
                    if i < 2:
                        last.then_inc(c_step, 1)
                        nc.vector.tensor_copy(part[:, :, :, :], part16[:, :, :, :]).then_inc(c_step, 1)
                        dve.wait_ge(c_step, n + 3)
                        nc.vector.tensor_tensor(slope[:, :, :, :], slope[:, :, :, :], part[:, :, :, :], ALU.subtract).then_inc(c_step, 1)
                    n += 4
                last.then_inc(c_ready, 1)
            ln.statistics(dve, 0)
            ln.normalise(dve, 0, xt_psum, DC)
            for i, (w, rows) in enumerate(((wq, DC), (wo, CH))):
                dve.wait_ge(w_hi, i + 1)
                raw = w_raw[:, 0:DC * QW].rearrange("p (c n) -> p c n", c=rows)
                nc.vector.tensor_tensor(w[1][:, :, :], raw, fp32_of(w[0][:, :, :]), ALU.subtract).then_inc(w_ready, 1)
            transposed_x(0)
            loop(dve, batch)

        @block.gpsimd
        def _(pool):
            poolt = Ticking(pool, m.sem("pool_ticks"))
            if not L0:
                pool.memset(w_rel[:, :], 0.0).then_inc(zeroed, 1)
                pool.memset(bias16[:, :, :, :], 0.0).then_inc(zeroed, 1)
            for v in vals:
                pool.memset(fp32_of(v[:, :]), 0.0).then_inc(zeroed, 1)
            pool.memset(prob[:, :, :], 0.0).then_inc(zeroed, 1)
            ZERO = 3 if L0 else 5

            def lay_out_keys(f, c):
                wait_apart(poolt, s_psum, HP * (f - 1) + (c + 1) * HP // KC)
                mask = head_mask[:, :].unsqueeze(2).to_broadcast([P, KH, SK])
                k = key[:, bass.ds(f, 1), :] if L0 else key[:, c, bass.ds(f, 1), :]
                nc.gpsimd.tensor_tensor(keys[:, c, :, :], k.to_broadcast([P, KH, SK]), mask, ALU.mult).then_inc(keys_ready, 1)

            def lay_out_values(g, c):
                wait_apart(poolt, pv_done, HP * (g - 1) + (c + 1) * HP // KC)
                if L0:
                    v = val[0:SK, bass.ds(g, 1), :].to_broadcast([SK, HC, dk])
                else:
                    v = val[0:SK, bass.ds(g, 1), c * P:(c + 1) * P].rearrange("p b (h e) -> p (b h) e", e=dk)
                hi, lo = (diagonal(tile, c) for tile in vals)
                nc.gpsimd.tensor_copy(hi, v).then_inc(vals_hi, 1)
                wait_apart(poolt, vals_hi, KC * g + c + 1)
                nc.gpsimd.tensor_tensor(lo, v, fp32_of(hi), ALU.subtract).then_inc(vals_ready, 1)

            def diagonal(v, c):
                return v[0:SK, c * HC * P:c * HC * P + HC * (P + dk)].rearrange("p (h n) -> p h n", n=P + dk)[:, :, 0:dk]

            def batch(f, front, back, following):
                g = f - 1
                if back:
                    lay_out_values(g, KC - 1)
                if front:
                    lay_out_keys(f, KC - 1)
                if front:
                    for t in range(HP):
                        wait_apart(poolt, inv_ready, HP * f + t + 1)
                        if back:
                            wait_apart(poolt, t_psum, HP * g + t + 1)
                        e = ex[t % RING][:, :, :].rearrange("p (q h) k -> p q h k", q=NC)
                        w = rinv[t % RING][:, :].rearrange("p (q h) -> p q h", q=NC).unsqueeze(3).to_broadcast([P, NC, 2, SK])
                        out = prob[:, :, t * PAIR:(t + 1) * PAIR].rearrange("p q (h k) -> p q h k", h=2)
                        nc.gpsimd.tensor_tensor(out, e, w, ALU.mult).then_inc(p_ready, 1)
                        if following and t == HP // 2 - 1:
                            ln.inverse_deviation(pool, f + 1)
                        if KC > 1 and t == HP // 2:
                            lay_out_values(f, 0)
                            if following:
                                lay_out_keys(f + 1, 0)

            ln.inverse_deviation(pool, 0)
            wait_apart(poolt, zeroed, ZERO)
            if KC > 1:
                lay_out_keys(0, 0)
            loop(pool, batch)


def ffn(nc, d, st):
    LAG = 2
    with ExitStack() as stack:
        m = Memory(nc, stack, "ffn")
        w_raw = m.sb("w_raw", [P, 2, 2048])
        w1 = m.split("w1", [P, DC, FC, P])
        w2 = m.split("w2", [P, FC, D])
        b1 = m.sb("b1", [P, FC])
        b2 = m.sb("b2", [P, D])
        ln = LayerNorm(nc, m, st)
        xT = m.split("xT", [P, DC, N])
        xb = m.sb("xb", [P, NC, D])
        RING = 3
        hid = [m.sb(f"hid{i}", [P, N]) for i in range(2)]
        hT = [m.split(f"hT{i}", [P, N]) for i in range(RING + 1)]
        h_bank = [m.ps(f"h_bank{i}") for i in range(4)]
        o_bank = [m.ps(f"o_bank{i}") for i in range(NC)]
        w_in = [m.sem("w1_in"), m.sem("w2_in")]
        w_hi, w_ready, b_in = m.sem("w_hi"), m.sem("w_ready"), m.sem("b_in")
        xt_psum, xt_hi, xt_lo = m.sem("xt_psum"), m.sem("xt_hi"), m.sem("xt_lo")
        h_psum, hid_ready, hid_hi, hid_lo = m.sem("h_psum"), m.sem("hid_ready"), m.sem("hid_hi"), m.sem("hid_lo")
        down_done, x_done, xb_ready = m.sem("down_done"), m.sem("x_done"), m.sem("xb_ready")
        stack.callback(m.end_phase)
        block = stack.enter_context(nc.Block())

        def raw_part(i, k):
            if i == 0:
                return w_raw[:, 0, k * FF:(k + 1) * FF].rearrange("p (j t) -> p t j", t=FC)
            return w_raw[:, 1, k * FF:(k + 1) * FF].rearrange("p (c n) -> p c n", n=D)

        def part_of(w, i, k):
            return w[:, k, :, :] if i == 0 else w[:, k * FC // 2:(k + 1) * FC // 2, :]

        def loop(eng, body):
            body(0, True)
            with eng.Fori(1, B - 1) as f:
                body(f, True)
            body(B - 1, False)

        @block.sync
        def _(sp):
            sp.dma_start(w_raw[:, 0, :].rearrange("p (c n) -> p c n", c=DC),
                         d["L0_ffn_w1"].rearrange("(c p) n -> p c n", p=P)).then_inc(w_in[0], 16)
            sp.dma_start(w_raw[:, 1, :].rearrange("p (c n) -> p c n", c=FC),
                         d["L0_ffn_w2"].rearrange("(p c) n -> p c n", p=P)).then_inc(w_in[1], 16)
            sp.dma_start(b1[:, :], d["L0_ffn_b1"].rearrange("(p c) -> p c", p=P)).then_inc(b_in, 16)
            sp.dma_start(b2[:, :], d["L0_ffn_b2"].rearrange("(a n) -> a n", a=1).broadcast_to([P, D])).then_inc(b_in, 16)

        @block.tensor
        def _(pe):
            def transpose_x(f):
                pe.wait_ge(ln.ready, NC * f + NC)
                for c in range(DC):
                    at_least(pe, xt_lo, DC * (f - 1) + c + 1)
                    for q in range(NC):
                        last = nc.tensor.transpose(h_bank[c][:, q * P:(q + 1) * P],
                                                   ln.xn[:, q, c * P:(c + 1) * P], st.ident[:, :])
                    last.then_inc(xt_psum, 1)

            def up(f, t):
                pe.wait_ge(xt_lo, DC * f + DC)
                at_least(pe, hid_ready, FC * f + t - 1)
                for n, (k, (a, b)) in enumerate((k, ab) for k in range(DC) for ab in PASSES):
                    last = nc.tensor.matmul(h_bank[2 + t % 2][:, 0:N], w1[a][:, k, t, :],
                                            xT[b][:, k, :], start=n == 0, stop=n == 5)
                last.then_inc(h_psum, 1)

            def down(f, t):
                pe.wait_ge(hid_lo, FC * f + t + 1)
                if t == 0:
                    at_least(pe, x_done, NC * f)
                h = hT[t % (RING + 1)]
                for q in range(NC):
                    for n, (a, b) in enumerate(PASSES):
                        last = nc.tensor.matmul(o_bank[q][:, 0:D], h[a][:, q * P:(q + 1) * P], w2[b][:, t, :],
                                                start=t == 0 and n == 0, stop=t == FC - 1 and n == 2)
                last.then_inc(down_done, 1)

            def batch(f, following):
                for t in range(FC):
                    up(f, t)
                    if t >= LAG:
                        down(f, t - LAG)
                if following:
                    transpose_x(f + 1)
                for t in range(FC - LAG, FC):
                    down(f, t)

            transpose_x(0)
            pe.wait_ge(w_ready, 2 * DC)
            loop(pe, batch)

        @block.scalar
        def _(act):
            def transposed_x(f):
                for c in range(DC):
                    act.wait_ge(xt_psum, DC * f + c + 1)
                    nc.scalar.copy(xT[0][:, c, :], h_bank[c][:, 0:N]).then_inc(xt_hi, 1)

            def batch(f, following):
                for t in range(FC):
                    act.wait_ge(h_psum, FC * f + t + 1)
                    at_least(act, hid_lo, FC * f + t - 1)
                    nc.scalar.activation(hid[t % 2][:, :], h_bank[2 + t % 2][:, 0:N], ACT.Gelu,
                                         bias=b1[:, t:t + 1]).then_inc(hid_ready, 1)
                if following:
                    transposed_x(f + 1)

            for i, w in enumerate((w1, w2)):
                act.wait_ge(w_in[i], 16)
                for k in range(DC):
                    nc.scalar.copy(part_of(w[0], i, k), raw_part(i, k)).then_inc(w_hi, 1)
            act.wait_ge(b_in, 32)
            transposed_x(0)
            loop(act, batch)

        @block.vector
        def _(dve):
            def transposed_x(f):
                for c in range(DC):
                    dve.wait_ge(xt_hi, DC * f + c + 1)
                    nc.vector.tensor_tensor(xT[1][:, c, :], h_bank[c][:, 0:N], fp32_of(xT[0][:, c, :]),
                                            ALU.subtract).then_inc(xt_lo, 1)

            def batch(f, following):
                for t in range(FC):
                    n = FC * f + t
                    h = hT[t % (RING + 1)]
                    dve.wait_ge(hid_ready, n + 1)
                    at_least(dve, down_done, n - RING)
                    nc.vector.tensor_copy(h[0][:, :], hid[t % 2][:, :]).then_inc(hid_hi, 1)
                    if t == 3 and following:
                        ln.normalise(dve, f + 1, xt_psum, DC)
                    dve.wait_ge(hid_hi, n + 1)
                    nc.vector.tensor_tensor(h[1][:, :], hid[t % 2][:, :], fp32_of(h[0][:, :]), ALU.subtract).then_inc(hid_lo, 1)
                    if t == 1 and following:
                        ln.statistics(dve, f + 1)
                if following:
                    transposed_x(f + 1)
                dve.wait_ge(xb_ready, f + 1)
                dve.wait_ge(down_done, FC * f + FC)
                for q in range(NC):
                    nc.vector.tensor_tensor(x_rows(st, f, q), o_bank[q][:, 0:D], xb[:, q, :], ALU.add).then_inc(x_done, 1)

            ln.statistics(dve, 0)
            ln.normalise(dve, 0, xt_psum, DC)
            for i, w in enumerate((w1, w2)):
                for k in range(DC):
                    dve.wait_ge(w_hi, DC * i + k + 1)
                    nc.vector.tensor_tensor(part_of(w[1], i, k), raw_part(i, k), fp32_of(part_of(w[0], i, k)),
                                            ALU.subtract).then_inc(w_ready, 1)
            transposed_x(0)
            loop(dve, batch)

        @block.gpsimd
        def _(pool):
            poolt = Ticking(pool, m.sem("pool_ticks"))
            def batch(f, following):
                if following:
                    ln.inverse_deviation(pool, f + 1)
                wait_apart(poolt, x_done, NC * f)
                nc.gpsimd.tensor_tensor(xb[:, :, :], st.x[:, bass.ds(f, 1), :, :].rearrange("p b q e -> p (b q) e"),
                                        b2[:, :].unsqueeze(1).to_broadcast([P, NC, D]), ALU.add).then_inc(xb_ready, 1)

            ln.inverse_deviation(pool, 0)
            wait_apart(poolt, b_in, 32)
            loop(pool, batch)


def batch_pairs(eng, body):
    body(0, 0, True, False, True)
    body(1, 1, True, True, True)
    body(2, 0, True, True, True)
    with eng.Fori(1, B // 2 - 1) as i:
        body(2 * i + 1, 1, True, True, True)
        body(2 * i + 2, 0, True, True, True)
    body(B - 1, 1, True, True, False)
    body(B, 0, False, True, False)


ES = E * S
EC = ES // P
NORM_EPS = 1e-12


def route(nc, d, st):
    with ExitStack() as stack:
        m = Memory(nc, stack, "route")
        gamma, beta = m.sb("gamma", [P, D]), m.sb("beta", [P, D])
        scale = m.sb("scale", [P, 1])
        mu_raw, mu_sq = m.sb("mu_raw", [P, DC, ES]), m.sb("mu_sq", [P, DC, ES])
        mu_norm, mu_inv, mu_unit = m.sb("mu_norm", [P, ES]), m.sb("mu_inv", [P, ES]), m.sb("mu_unit", [P, DC, ES])
        mu = m.split("mu", [P, DC, ES])
        ones = m.sb("ones", [P, P])
        half = m.sb("half", [P, ES])
        ln = LayerNorm(nc, m, st)
        xg = m.sb("xg", [P, NC, D])
        xa = m.sb("xa", [P, NC, D])
        sq = m.sb("sq", [P, D])
        sumsq, length, length_min, inv_length = (m.sb(n, [P, NC]) for n in ("sumsq", "length", "length_min", "inv_length"))
        xu = m.sb("xu", [P, NC, D])
        xaS = [m.split(f"xaS{i}", [P, NC, D]) for i in range(2)]
        xT = m.split("xT", [P, DC, N])
        top = [m.sb(f"top{k}", [P, 2]) for k in range(2)]
        ex = [m.sb(f"ex{k}", [P, 2, ES]) for k in range(2)]
        rsum = [m.sb(f"rsum{k}", [P, 2]) for k in range(2)]
        rinv = [m.sb(f"rinv{k}", [P, 2]) for k in range(2)]
        weight = [m.sb(f"weight{k}", [P, 2, ES]) for k in range(2)]
        disp = m.split("disp", [P, NC, ES])
        x_bank = [m.ps(f"x_bank{c}") for c in range(DC)]
        l_bank = [m.ps(f"l_bank{k}") for k in range(2)]
        t_bank = [m.ps(f"t_bank{k}") for k in range(2)]
        i_bank = m.ps("i_bank")

        in_, mu_in = m.sem("small_in"), m.sem("mu_in")
        const_ready, mu_step, mu_psum, mu_ready = m.sem("const_ready"), m.sem("mu_step"), m.sem("mu_psum"), m.sem("mu_ready")
        mu_pow = m.sem("mu_pow")
        xg_ready, xa_ready, sq_step, sumsq_ready = m.sem("xg_ready"), m.sem("xa_ready"), m.sem("sq_step"), m.sem("sumsq_ready")
        len_ready, lmin_ready, inv_ready, xu_ready = m.sem("len_ready"), m.sem("lmin_ready"), m.sem("inv_ready"), m.sem("xu_ready")
        xas_hi, xas_ready = m.sem("xas_hi"), m.sem("xas_ready")
        xt_psum, xt_hi, xt_lo = m.sem("xt_psum"), m.sem("xt_hi"), m.sem("xt_lo")
        l_psum, top_ready, ex_ready = m.sem("l_psum"), m.sem("top_ready"), m.sem("ex_ready")
        rinv_ready, weight_ready = m.sem("rinv_ready"), m.sem("weight_ready")
        t_psum, comb_stored, disp_hi, disp_lo = m.sem("t_psum"), m.sem("comb_stored"), m.sem("disp_hi"), m.sem("disp_lo")
        i_psum, slots_stored = m.sem("i_psum"), m.sem("slots_stored")
        stack.callback(m.end_phase)
        block = stack.enter_context(nc.Block())

        @block.sync
        def _(sp):
            sp.dma_start(mu_raw[:, :, :], d["L1_ffn_mu"].rearrange("(c p) e s -> p c (e s)", p=P)).then_inc(mu_in, 16)
            row = lambda name: d[name].rearrange("(a n) -> a n", a=1)
            sp.dma_start(gamma[:, :], row("L1_ffn_ln_gamma").broadcast_to([P, D])).then_inc(in_, 16)
            sp.dma_start(beta[:, :], row("L1_ffn_ln_beta").broadcast_to([P, D])).then_inc(in_, 16)
            sp.dma_start(scale[:, :], row("L1_ffn_scale").broadcast_to([P, 1])).then_inc(in_, 16)

        @block.tensor
        def _(pe):
            def transpose_x(f):
                pe.wait_ge(xu_ready, NC * f + NC)
                for c in range(DC):
                    at_least(pe, xt_lo, DC * (f - 1) + c + 1)
                    for q in range(NC):
                        last = nc.tensor.transpose(x_bank[c][:, q * P:(q + 1) * P],
                                                   xu[:, q, c * P:(c + 1) * P], st.ident[:, :])
                    last.then_inc(xt_psum, 1)

            def logits(f):
                pe.wait_ge(xt_lo, DC * f + DC)
                for k in range(2):
                    at_least(pe, ex_ready, 4 * (f - 1) + 2 * k + 2)
                    rows, cols = ((xT, mu), (mu, xT))[k]
                    for r in range(2):
                        for n, (c, (a, b)) in enumerate((c, ab) for c in range(DC) for ab in PASSES):
                            last = nc.tensor.matmul(l_bank[k][:, r * ES:(r + 1) * ES], rows[a][:, c, r * P:(r + 1) * P],
                                                    cols[b][:, c, :], start=n == 0, stop=n == 5)
                    last.then_inc(l_psum, 1)

            def transpose_weights(g):
                for k in range(2):
                    pe.wait_ge(weight_ready, 4 * g + 2 * k + 2)
                    at_least(pe, (comb_stored, disp_lo)[k], g)
                    for r in range(2):
                        for j in range(2):
                            last = nc.tensor.transpose(t_bank[k][:, j * ES + r * P:j * ES + (r + 1) * P],
                                                       weight[k][:, r, j * P:(j + 1) * P], st.ident[:, :])
                    last.then_inc(t_psum, 1)

            def slot_inputs(g, i):
                pe.wait_ge(disp_lo, g + 1)
                pe.wait_ge(xas_ready, g + 1)
                at_least(pe, slots_stored, g)
                for c in range(DC):
                    for n, (q, (a, b)) in enumerate((q, ab) for q in range(NC) for ab in PASSES):
                        last = nc.tensor.matmul(i_bank[:, c * ES:(c + 1) * ES], xaS[i][a][:, q, c * P:(c + 1) * P],
                                                disp[b][:, q, :], start=n == 0, stop=n == 5)
                last.then_inc(i_psum, 1)

            def batch(f, i, front, back, following):
                if front:
                    logits(f)
                if back:
                    transpose_weights(f - 1)
                if following:
                    transpose_x(f + 1)
                if back:
                    slot_inputs(f - 1, 1 - i)

            pe.wait_ge(const_ready, 2)
            pe.wait_ge(mu_step, 1)
            for c in range(DC):
                last = nc.tensor.matmul(i_bank[:, 0:ES], ones[:, :], mu_sq[:, c, :], start=c == 0, stop=c == DC - 1)
            last.then_inc(mu_psum, 1)
            transpose_x(0)
            pe.wait_ge(mu_ready, 1)
            batch_pairs(pe, batch)

        @block.scalar
        def _(act):
            def square(f):
                act.wait_ge(xa_ready, f + 1)
                for q in range(NC):
                    at_least(act, sumsq_ready, NC * f + q)
                    at_least(act, len_ready, f)
                    nc.scalar.activation(sq[:, :], xa[:, q, :], ACT.Square, accum_out=sumsq[:, q:q + 1]).then_inc(sumsq_ready, 1)

            def transposed_x(f):
                for c in range(DC):
                    act.wait_ge(xt_psum, DC * f + c + 1)
                    at_least(act, l_psum, 2 * f)
                    nc.scalar.copy(xT[0][:, c, :], x_bank[c][:, 0:N]).then_inc(xt_hi, 1)

            def exponentials(f):
                for k in range(2):
                    act.wait_ge(top_ready, 2 * f + k + 1)
                    at_least(act, weight_ready, 4 * (f - 1) + 2 * k + 2)
                    for r in range(2):
                        nc.scalar.activation(ex[k][:, r, :], l_bank[k][:, r * ES:(r + 1) * ES], ACT.Exp,
                                             bias=top[k][:, r:r + 1], accum_out=rsum[k][:, r:r + 1]).then_inc(ex_ready, 1)

            def batch(f, i, front, back, following):
                g = f - 1
                if front:
                    exponentials(f)
                if back:
                    act.wait_ge(t_psum, 2 * g + 1)
                    nc.scalar.copy(st.comb[:, :, bass.ds(g, 1), :].rearrange("p j b n -> p (j b) n"),
                                   t_bank[0][:, :].rearrange("p (j n) -> p j n", j=EC)).then_inc(comb_stored, 1)
                    act.wait_ge(t_psum, 2 * g + 2)
                    at_least(act, i_psum, g)
                    nc.scalar.copy(disp[0][:, :, :], t_bank[1][:, :].rearrange("p (q n) -> p q n", q=NC)).then_inc(disp_hi, 1)
                if following:
                    square(f + 1)
                    transposed_x(f + 1)
                if back:
                    act.wait_ge(i_psum, g + 1)
                    nc.scalar.copy(st.slots[:, :, bass.ds(g, 1), :].rearrange("p c b n -> p (c b) n"),
                                   i_bank[:, :].rearrange("p (c n) -> p c n", c=DC)).then_inc(slots_stored, 1)

            square(0)
            transposed_x(0)
            batch_pairs(act, batch)

        @block.vector
        def _(dve):
            def unit(f):
                dve.wait_ge(lmin_ready, f + 1)
                at_least(dve, xu_ready, NC * f)
                nc.vector.reciprocal(inv_length[:, :], length_min[:, :]).then_inc(inv_ready, 1)
                dve.wait_ge(inv_ready, f + 1)
                at_least(dve, xt_psum, DC * f)
                for q in range(NC):
                    nc.vector.tensor_scalar(xu[:, q, :], xa[:, q, :], inv_length[:, q:q + 1], scale[:, 0:1],
                                            ALU.mult, ALU.mult).then_inc(xu_ready, 1)

            def transposed_x(f):
                for c in range(DC):
                    dve.wait_ge(xt_hi, DC * f + c + 1)
                    nc.vector.tensor_tensor(xT[1][:, c, :], x_bank[c][:, 0:N], fp32_of(xT[0][:, c, :]),
                                            ALU.subtract).then_inc(xt_lo, 1)

            def batch(f, i, front, back, following):
                g = f - 1
                if front:
                    for k in range(2):
                        dve.wait_ge(l_psum, 2 * f + k + 1)
                        nc.vector.tensor_reduce(top[k][:, :], l_bank[k][:, :].rearrange("p (r n) -> p r n", r=2), AX,
                                                ALU.max, negate=True).then_inc(top_ready, 1)
                if following:
                    ln.statistics(dve, f + 1)
                    ln.normalise(dve, f + 1, xg_ready, 1)
                if back:
                    dve.wait_ge(disp_hi, g + 1)
                    nc.vector.tensor_tensor(disp[1][:, :, :], t_bank[1][:, :].rearrange("p (q n) -> p q n", q=NC),
                                            fp32_of(disp[0][:, :, :]), ALU.subtract).then_inc(disp_lo, 1)
                if front:
                    for k in range(2):
                        dve.wait_ge(ex_ready, 4 * f + 2 * k + 2)
                        nc.vector.reciprocal(rinv[k][:, :], rsum[k][:, :]).then_inc(rinv_ready, 1)
                    for k in range(2):
                        dve.wait_ge(rinv_ready, 2 * f + k + 1)
                        at_least(dve, t_psum, 2 * g + k + 1)
                        for r in range(2):
                            nc.vector.tensor_scalar(weight[k][:, r, :], ex[k][:, r, :], rinv[k][:, r:r + 1], None,
                                                    ALU.mult).then_inc(weight_ready, 1)
                if following:
                    unit(f + 1)
                    transposed_x(f + 1)

            dve.wait_ge(mu_in, 16)
            nc.vector.tensor_tensor(mu_sq[:, :, :], mu_raw[:, :, :], mu_raw[:, :, :], ALU.mult).then_inc(mu_step, 1)
            ln.statistics(dve, 0)
            ln.normalise(dve, 0, xg_ready, 1)
            dve.wait_ge(mu_psum, 1)
            nc.vector.tensor_copy(mu_norm[:, :], i_bank[:, 0:ES]).then_inc(mu_step, 1)
            dve.wait_ge(mu_pow, 2)
            nc.vector.reciprocal(mu_inv[:, :], mu_norm[:, :]).then_inc(mu_step, 1)
            dve.wait_ge(mu_step, 3)
            nc.vector.tensor_tensor(mu_unit[:, :, :], mu_raw[:, :, :], mu_inv[:, :].unsqueeze(1).to_broadcast([P, DC, ES]),
                                    ALU.mult).then_inc(mu_step, 1)
            dve.wait_ge(mu_step, 4)
            nc.vector.tensor_copy(mu[0][:, :, :], mu_unit[:, :, :]).then_inc(mu_step, 1)
            dve.wait_ge(mu_step, 5)
            nc.vector.tensor_tensor(mu[1][:, :, :], mu_unit[:, :, :], fp32_of(mu[0][:, :, :]), ALU.subtract).then_inc(mu_ready, 1)
            dve.wait_ge(in_, 48)
            unit(0)
            transposed_x(0)
            batch_pairs(dve, batch)

        @block.gpsimd
        def _(pool):
            poolt = Ticking(pool, m.sem("pool_ticks"))
            def affine(f):
                wait_apart(poolt, ln.ready, NC * f + NC)
                wait_apart(poolt, xa_ready, f)
                nc.gpsimd.tensor_tensor(xg[:, :, :], ln.xn[:, :, :], gamma[:, :].unsqueeze(1).to_broadcast([P, NC, D]),
                                        ALU.mult).then_inc(xg_ready, 1)
                wait_apart(poolt, xg_ready, f + 1)
                wait_apart(poolt, xu_ready, NC * f)
                wait_apart(poolt, xas_ready, f)
                nc.gpsimd.tensor_tensor(xa[:, :, :], xg[:, :, :], beta[:, :].unsqueeze(1).to_broadcast([P, NC, D]),
                                        ALU.add).then_inc(xa_ready, 1)

            def lengths(f):
                wait_apart(poolt, sumsq_ready, NC * f + NC)
                wait_apart(poolt, lmin_ready, f)
                nc.gpsimd.tensor_tensor(length[:, :], sumsq[:, :], half[:, 0:NC], ALU.pow).then_inc(len_ready, 1)
                wait_apart(poolt, len_ready, f + 1)
                wait_apart(poolt, inv_ready, f)
                nc.gpsimd.tensor_scalar(length_min[:, :], length[:, :], NORM_EPS, None, ALU.max).then_inc(lmin_ready, 1)

            def split_x(f, i):
                wait_apart(poolt, xa_ready, f + 1)
                wait_apart(poolt, i_psum, f - 1)
                nc.gpsimd.tensor_copy(xaS[i][0][:, :, :], xa[:, :, :]).then_inc(xas_hi, 1)
                wait_apart(poolt, xas_hi, f + 1)
                nc.gpsimd.tensor_tensor(xaS[i][1][:, :, :], xa[:, :, :], fp32_of(xaS[i][0][:, :, :]),
                                        ALU.subtract).then_inc(xas_ready, 1)

            def batch(f, i, front, back, following):
                if following:
                    ln.inverse_deviation(pool, f + 1)
                    affine(f + 1)
                    lengths(f + 1)
                    split_x(f + 1, 1 - i)

            pool.memset(ones[:, :], 1.0).then_inc(const_ready, 1)
            pool.memset(half[:, :], 0.5).then_inc(const_ready, 1)
            ln.inverse_deviation(pool, 0)
            wait_apart(poolt, in_, 48)
            affine(0)
            wait_apart(poolt, mu_step, 2)
            wait_apart(poolt, const_ready, 2)
            nc.gpsimd.tensor_tensor(mu_inv[:, :], mu_norm[:, :], half[:, :], ALU.pow).then_inc(mu_pow, 1)
            wait_apart(poolt, mu_pow, 1)
            nc.gpsimd.tensor_scalar(mu_norm[:, :], mu_inv[:, :], NORM_EPS, None, ALU.max).then_inc(mu_pow, 1)
            lengths(0)
            split_x(0, 0)
            batch_pairs(pool, batch)


def experts(nc, d, st):
    with ExitStack() as stack:
        m = Memory(nc, stack, "exp")
        b_raw = m.sb("b_raw", [E, HID + D])
        b1, b2 = m.sb("b1", [HID, E]), m.sb("b2", [P, DC, E])
        w1_raw = [m.sb(f"w1_raw{i}", [P, DC, HID]) for i in range(2)]
        w2_raw = [m.sb(f"w2_raw{i}", [HID, D]) for i in range(2)]
        w1 = [m.split(f"w1_{i}", [P, DC, HID]) for i in range(2)]
        w2 = [m.split(f"w2_{i}", [HID, D]) for i in range(2)]
        xin = [m.split(f"xin{i}", [P, DC, B, S]) for i in range(2)]
        hid = [m.sb(f"hid{i}", [HID, B * S]) for i in range(2)]
        hT = [m.split(f"hT{i}", [HID, B * S]) for i in range(2)]
        b_bank = m.ps("b_bank")
        h_bank = [m.ps(f"h_bank{i}") for i in range(2)]
        o_bank = [m.ps(f"o_bank{i}") for i in range(2)]
        b_in, b_psum, b_ready = m.sem("b_in"), m.sem("b_psum"), m.sem("b_ready")
        w_in = [m.sem(f"w_in{i}") for i in range(2)]
        hi_ready, lo_ready = m.sem("hi_ready"), m.sem("lo_ready")
        h_psum, hid_ready, hid_hi, hid_lo = m.sem("h_psum"), m.sem("hid_ready"), m.sem("hid_hi"), m.sem("hid_lo")
        o_psum, out_stored = m.sem("o_psum"), m.sem("out_stored")
        stack.callback(m.end_phase)
        block = stack.enter_context(nc.Block())

        def slots_of(e):
            return st.slots[:, :, :, bass.ds(e * S, S)]

        @block.sync
        def _(sp):
            sp.dma_start(b_raw[:, 0:HID], d["L1_ffn_b1"]).then_inc(b_in, 16)
            sp.dma_start(b_raw[:, HID:], d["L1_ffn_b2"]).then_inc(b_in, 16)

            def load(e, i):
                sp.dma_start(w1_raw[i][:, :, :], d["L1_ffn_w1"][bass.ds(e, 1)].rearrange("a (c p) h -> p (a c) h", p=P)).then_inc(w_in[i], 16)
                sp.dma_start(w2_raw[i][:, :], d["L1_ffn_w2"][bass.ds(e, 1)].rearrange("a h n -> (a h) n")).then_inc(w_in[i], 16)

            for i in range(2):
                load(i, i)
            with sp.Fori(1, E // 2) as k:
                for i in range(2):
                    sp.wait_ge(lo_ready, 2 * k + i - 1)
                    load(2 * k + i, i)

        @block.tensor
        def _(pe):
            def up(e, i):
                pe.wait_ge(lo_ready, e + 1)
                at_least(pe, hid_ready, e - 1)
                for n, (c, (a, b)) in enumerate((c, ab) for c in range(DC) for ab in PASSES):
                    last = nc.tensor.matmul(h_bank[i][0:HID, 0:B * S], w1[i][a][:, c, :], xin[i][b][:, c, :, :],
                                            start=n == 0, stop=n == 5)
                last.then_inc(h_psum, 1)

            def down(e, i):
                pe.wait_ge(hid_lo, e + 1)
                at_least(pe, out_stored, DC * (e - 1))
                for c in range(DC):
                    for n, (a, b) in enumerate(PASSES):
                        last = nc.tensor.matmul(o_bank[i][:, c * B * S:(c + 1) * B * S], w2[i][a][:, c * P:(c + 1) * P],
                                                hT[i][b][:, :], start=n == 0, stop=n == 2)
                last.then_inc(o_psum, 1)

            def step(e, i, front, back, following):
                if front:
                    up(e, i)
                if back:
                    down(e - 1, 1 - i)

            pe.wait_ge(b_in, 32)
            nc.tensor.transpose(b_bank[0:HID, 0:E], b_raw[:, 0:HID], st.ident[0:E, 0:E])
            for c in range(DC):
                last = nc.tensor.transpose(b_bank[:, (c + 1) * E:(c + 2) * E], b_raw[:, HID + c * P:HID + (c + 1) * P],
                                           st.ident[0:E, 0:E])
            last.then_inc(b_psum, 1)
            batch_pairs(pe, step)

        @block.scalar
        def _(act):
            def split(e, i):
                act.wait_ge(w_in[i], 32 * ((e - i) // 2 + 1) if isinstance(e, int) else 16 * (e - i) + 32)
                at_least(act, h_psum, e - 1)
                nc.scalar.copy(w1[i][0][:, :, :], w1_raw[i][:, :, :])
                at_least(act, o_psum, e - 1)
                nc.scalar.copy(w2[i][0][:, :], w2_raw[i][:, :])
                nc.scalar.copy(xin[i][0][:, :, :, :], slots_of(e)).then_inc(hi_ready, 1)

            def step(e, i, front, back, following):
                if front:
                    act.wait_ge(h_psum, e + 1)
                    at_least(act, hid_lo, e - 1)
                    nc.scalar.activation(hid[i][:, :], h_bank[i][0:HID, 0:B * S], ACT.Gelu,
                                         bias=b1[:, bass.ds(e, 1)]).then_inc(hid_ready, 1)
                if following:
                    split(e + 1, 1 - i)
                if back:
                    act.wait_ge(o_psum, e)
                    for c in range(DC):
                        act.wait_ge(lo_ready, e)
                        out = st.slots[:, c, :, bass.ds((e - 1) * S, S)]
                        nc.scalar.activation(out, o_bank[1 - i][:, c * B * S:(c + 1) * B * S].rearrange("p (b s) -> p b s", b=B),
                                             ACT.Identity, bias=b2[:, c, bass.ds(e - 1, 1)]).then_inc(out_stored, 1)

            split(0, 0)
            act.wait_ge(b_ready, 2)
            batch_pairs(act, step)

        @block.vector
        def _(dve):
            def split(e, i):
                dve.wait_ge(hi_ready, e + 1)
                nc.vector.tensor_tensor(w1[i][1][:, :, :], w1_raw[i][:, :, :], fp32_of(w1[i][0][:, :, :]), ALU.subtract)
                nc.vector.tensor_tensor(w2[i][1][:, :], w2_raw[i][:, :], fp32_of(w2[i][0][:, :]), ALU.subtract)
                for c in range(DC):
                    last = nc.vector.tensor_tensor(xin[i][1][:, c, :, :], st.slots[:, c, :, bass.ds(e * S, S)],
                                                   fp32_of(xin[i][0][:, c, :, :]), ALU.subtract)
                last.then_inc(lo_ready, 1)

            def step(e, i, front, back, following):
                if following:
                    split(e + 1, 1 - i)
                if front:
                    dve.wait_ge(hid_ready, e + 1)
                    at_least(dve, o_psum, e - 1)
                    nc.vector.tensor_copy(hT[i][0][:, :], hid[i][:, :]).then_inc(hid_hi, 1)
                    dve.wait_ge(hid_hi, e + 1)
                    nc.vector.tensor_tensor(hT[i][1][:, :], hid[i][:, :], fp32_of(hT[i][0][:, :]), ALU.subtract).then_inc(hid_lo, 1)

            split(0, 0)
            dve.wait_ge(b_psum, 1)
            nc.vector.tensor_copy(b1[:, :], b_bank[0:HID, 0:E]).then_inc(b_ready, 1)
            nc.vector.tensor_copy(b2[:, :, :], b_bank[:, E:(DC + 1) * E].rearrange("p (c e) -> p c e", c=DC)).then_inc(b_ready, 1)
            batch_pairs(dve, step)


def combine(nc, d, st, out):
    with ExitStack() as stack:
        m = Memory(nc, stack, "comb")
        so = [m.sb(f"so{i}", [P, DC, ES]) for i in range(2)]
        soS = [m.split(f"soS{i}", [P, EC, D]) for i in range(2)]
        cT = [m.split(f"cT{i}", [P, EC, N]) for i in range(2)]
        y = [m.sb(f"y{i}", [P, NC, D]) for i in range(2)]
        s_bank = [m.ps(f"s_bank{i}") for i in range(2)]
        y_bank = [m.ps(f"y_bank{i}") for i in range(2)]
        so_ready, s_psum, so_hi, so_lo = m.sem("so_ready"), m.sem("s_psum"), m.sem("so_hi"), m.sem("so_lo")
        ct_hi, ct_lo, y_psum, y_ready = m.sem("ct_hi"), m.sem("ct_lo"), m.sem("y_psum"), m.sem("y_ready")
        y_out = [m.sem(f"y_out{i}") for i in range(2)]
        stack.callback(m.end_phase)
        block = stack.enter_context(nc.Block())

        @block.sync
        def _(sp):
            def store(f, i):
                sp.wait_ge(y_ready, f + 1)
                sp.dma_start(out[bass.ds(f, 1)].rearrange("b (q p) n -> p (b q) n", p=P), y[i][:, :, :]).then_inc(y_out[i], 16)

            with sp.Fori(0, B // 2) as k:
                for i in range(2):
                    store(2 * k + i, i)
            for i in range(2):
                sp.wait_ge(y_out[i], 16 * (B // 2))

        @block.tensor
        def _(pe):
            def step(f, i, front, back, following):
                g = f - 1
                if front:
                    pe.wait_ge(so_ready, f + 1)
                    at_least(pe, so_lo, f - 1)
                    for c in range(DC):
                        for j in range(EC):
                            last = nc.tensor.transpose(s_bank[i][:, j * D + c * P:j * D + (c + 1) * P],
                                                       so[i][:, c, j * P:(j + 1) * P], st.ident[:, :])
                    last.then_inc(s_psum, 1)
                if back:
                    pe.wait_ge(so_lo, g + 1)
                    pe.wait_ge(ct_lo, g + 1)
                    at_least(pe, y_ready, g - 1)
                    for q in range(NC):
                        for n, (j, (a, b)) in enumerate((j, ab) for j in range(EC) for ab in PASSES):
                            last = nc.tensor.matmul(y_bank[1 - i][:, q * D:(q + 1) * D], cT[1 - i][a][:, j, q * P:(q + 1) * P],
                                                    soS[1 - i][b][:, j, :], start=n == 0, stop=n == 5)
                    last.then_inc(y_psum, 1)

            batch_pairs(pe, step)

        @block.scalar
        def _(act):
            def step(f, i, front, back, following):
                if front:
                    at_least(act, y_psum, f - 1)
                    nc.scalar.copy(cT[i][0][:, :, :], st.comb[:, :, bass.ds(f, 1), :].rearrange("p j b n -> p (j b) n")).then_inc(ct_hi, 1)
                    act.wait_ge(s_psum, f + 1)
                    nc.scalar.copy(soS[i][0][:, :, :], s_bank[i][:, :].rearrange("p (j n) -> p j n", j=EC)).then_inc(so_hi, 1)

            batch_pairs(act, step)

        @block.vector
        def _(dve):
            def fetch(f, i):
                at_least(dve, s_psum, f - 1)
                nc.vector.tensor_copy(so[i][:, :, :], st.slots[:, :, bass.ds(f, 1), :].rearrange("p c b n -> p (c b) n")).then_inc(so_ready, 1)

            def step(f, i, front, back, following):
                g = f - 1
                if following:
                    fetch(f + 1, 1 - i)
                if front:
                    dve.wait_ge(so_hi, f + 1)
                    nc.vector.tensor_tensor(soS[i][1][:, :, :], s_bank[i][:, :].rearrange("p (j n) -> p j n", j=EC),
                                            fp32_of(soS[i][0][:, :, :]), ALU.subtract).then_inc(so_lo, 1)
                if back:
                    dve.wait_ge(y_psum, g + 1)
                    if isinstance(g, int):
                        at_least(dve, y_out[1 - i], 16 * (g // 2))
                    else:
                        dve.wait_ge(y_out[1 - i], 8 * (g - (1 - i)))
                    nc.vector.tensor_tensor(y[1 - i][:, :, :], y_bank[1 - i][:, :].rearrange("p (q n) -> p q n", q=NC),
                                            st.x[:, bass.ds(g, 1), :, :].rearrange("p b q n -> p (b q) n"), ALU.add).then_inc(y_ready, 1)

            fetch(0, 0)
            batch_pairs(dve, step)

        @block.gpsimd
        def _(pool):
            poolt = Ticking(pool, m.sem("pool_ticks"))
            def step(f, i, front, back, following):
                if front:
                    wait_apart(poolt, ct_hi, f + 1)
                    nc.gpsimd.tensor_tensor(cT[i][1][:, :, :], st.comb[:, :, bass.ds(f, 1), :].rearrange("p j b n -> p (j b) n"),
                                            fp32_of(cT[i][0][:, :, :]), ALU.subtract).then_inc(ct_lo, 1)

            batch_pairs(pool, step)


def moe(nc, d, st, out):
    with ExitStack() as stack:
        m = Memory(nc, stack, "moe")
        st.slots = m.sb("slots", [P, DC, B, ES])
        st.comb = m.sb("comb", [P, EC, B, N])
        route(nc, d, st)
        experts(nc, d, st)
        combine(nc, d, st, out)


class Store:
    pass


def build(nc, d, out, last_phase=5):
    with ExitStack() as stack:
        m = Memory(nc, stack, "all")
        st = Store()
        st.x = m.sb("x", [P, B, NC, D])
        st.ident = m.sb("ident", [P, P])
        st.minus_half = m.sb("minus_half", [P, NC])
        st.head_mask0 = m.sb("head_mask0", [P, 2])
        st.head_mask1 = m.sb("head_mask1", [P, 8])
        with ExitStack() as kv_stack:
            kv = Memory(nc, kv_stack, "kv")
            st.key0 = kv.sb("key0", [P, B, SK])
            st.key1 = kv.sb("key1", [P, DC, B, SK])
            st.val0 = kv.sb("val0", [P, B, DK0])
            st.val1 = kv.sb("val1", [P, B, D])
            prologue(nc, d, st)
            if last_phase >= 1:
                attention(nc, d, st, 0)
            if last_phase >= 2:
                ffn(nc, d, st)
            if last_phase >= 3:
                attention(nc, d, st, 1)
        if last_phase >= 4:
            moe(nc, d, st, out)
        else:
            o_out = m.sem("o_out")
            block = stack.enter_context(nc.Block())

            @block.sync
            def _(sp):
                for b in range(B):
                    sp.dma_start(out[b].rearrange("(q p) e -> p q e", p=P), st.x[:, b, :, :]).then_inc(o_out, 16)
                sp.wait_ge(o_out, 16 * B)


def constants():
    p = np.arange(P)
    rows = np.isin(p, (0, 32, 64)).astype(np.float32)
    positions = np.stack([rows[:, None] * np.arange(N, dtype=np.float32), rows[:, None] * np.ones(N, np.float32)], 1)
    causal = np.where(p[:, None] >= np.arange(SK)[None, :], 0.0, -1e9).astype(np.float32)
    return {
        "ident": np.eye(P, dtype=np.float32),
        "head_mask0": (p[:, None] // DK0 == np.arange(P // DK0)).astype(np.float32),
        "head_mask1": (p[:, None] // DK1 == np.arange(P // DK1)).astype(np.float32),
        "causal": np.concatenate([causal, causal], 1),
        "positions": positions.astype(np.float32),
        "neg_k": np.broadcast_to(-np.arange(SK, dtype=np.float32), (P, SK)).copy(),
    }


def kernel(**inputs):
    import concourse.bacc as bacc
    from concourse.bass_utils import run_bass_kernel_spmd

    nc = bacc.Bacc("TRN2", target_bir_lowering=False, num_devices=1)
    arrays, d = {}, {}
    for name, a in {**inputs, **constants()}.items():
        a = np.ascontiguousarray(a)
        arrays[f"in_{name}"] = a
        d["ctx" if name == "ctx_1024" else name] = nc.dram_tensor(
            f"in_{name}", a.shape, mybir.dt.from_np(a.dtype), kind="ExternalInput").ap()
    out = nc.dram_tensor("out", (B, N, D), F32, kind="ExternalOutput").ap()
    build(nc, d, out)
    r = run_bass_kernel_spmd(nc, [arrays], core_ids=[0])
    return r.results[0]["out"]
```

```python
from contextlib import ExitStack

import numpy as np
import concourse.bass as bass
from concourse import mybir

ALU = mybir.AluOpType
ACT = mybir.ActivationFunctionType
AX = mybir.AxisListType.X
F32 = mybir.dt.float32
F32R = mybir.dt.float32r
BF16 = mybir.dt.bfloat16

P = 128
B = 16
N = 256
NC = N // P
D = 256
DC = D // P
SK = 77
H = 16
HP = H // 2
PAIR = 2 * SK
DK0 = 64
DK1 = 16
FF = 1024
FC = FF // P
E = 16
S = 16
HID = 64
LN_EPS = 1e-5
PASSES = ((0, 0), (0, 1), (1, 0))


def at_least(eng, sem, value):
    if not isinstance(value, int) or value > 0:
        eng.wait_ge(sem, value)


def wait_apart(eng, sem, value):
    at_least(eng.engine, sem, value)
    if not isinstance(value, int):
        eng.engine.sem_inc(eng.ticks, 1)


class Ticking:

    def __init__(self, engine, ticks):
        self.engine, self.ticks = engine, ticks


def fp32_of(ap):
    return ap.bitcast(F32)


class Memory:

    def __init__(self, nc, stack, prefix):
        self.nc, self.stack, self.prefix, self.sems = nc, stack, prefix, []

    def sb(self, name, shape, dt=F32):
        return self.stack.enter_context(self.nc.sbuf_tensor(f"{self.prefix}_{name}", shape, dt))

    def ps(self, name, cols=512, dt=F32):
        return self.stack.enter_context(self.nc.psum_tensor(f"{self.prefix}_{name}", [P, cols], dt))

    def sem(self, name):
        self.sems.append(self.nc.alloc_semaphore(f"{self.prefix}_{name}"))
        return self.sems[-1]

    def end_phase(self):
        self.nc.clear_and_free_semaphores(self.sems)
        self.nc.all_engine_barrier()

    def split(self, name, shape):
        return self.sb(name + "_hi", shape, F32R), self.sb(name + "_lo", shape, F32R)


def load_raw(sp, d, st, names, sem):
    at = 0
    for name in names:
        w = d[name].rearrange("(p c) n -> p c n", p=P) if name == "L0_ffn_w2" else \
            d[name].rearrange("(c p) e s -> p c (e s)", p=P) if name == "L1_ffn_mu" else \
            d[name].rearrange("(c p) n -> p c n", p=P)
        c, n = w.shape[1:]
        sp.dma_start(st.raw[:, at:at + c * n].rearrange("p (c n) -> p c n", c=c), w).then_inc(sem, 16)
        at += c * n


def prologue(nc, d, st):
    G = 4
    GK = G * SK
    VC = DK0 + D
    with ExitStack() as stack:
        m = Memory(nc, stack, "pro")
        w_raw = m.sb("w_raw", [P, DC, 2 * DK0 + 2 * D])
        wk = m.split("wk", [P, DC, P + D])
        wv = m.split("wv", [P, DC, VC])
        ctx_in = m.sb("ctx_in", [SK, G, D])
        ctxT = m.split("ctxT", [P, DC, GK])
        ctxT_ps = [m.ps(f"ctxT_ps{c}") for c in range(DC)]
        key_ps = [m.ps(f"key_ps{j}") for j in range(3)]
        val_ps = [m.ps(f"val_ps{j}") for j in range(2)]
        x_in = m.sem("x_in")
        half_ready = m.sem("half_ready")
        const_in = m.sem("const_in")
        w_in = m.sem("w_in")
        ctx_read, raw_in = m.sem("ctx_read"), m.sem("raw_in")
        wk_ready, wv_ready, whi = m.sem("wk_ready"), m.sem("wv_ready"), m.sem("whi")
        ctxT_psum, ctxT_hi, ctxT_lo = m.sem("ctxT_psum"), m.sem("ctxT_hi"), m.sem("ctxT_lo")
        key_psum, key_done = m.sem("key_psum"), m.sem("key_done")
        val_psum, val_done = m.sem("val_psum"), m.sem("val_done")
        stack.callback(m.end_phase)
        block = stack.enter_context(nc.Block())

        @block.sync
        def _(sp):
            sp.dma_start(st.ident[:, :], d["ident"]).then_inc(const_in, 16)
            sp.dma_start(ctx_in[:, :, :], d["ctx"][0:G].rearrange("b k e -> k b e")).then_inc(ctx_read, 16)
            sp.dma_start(w_raw[:, :, 0:DK0], d["L0_xattn_W_k"].rearrange("(c p) n -> p c n", p=P)).then_inc(w_in, 16)
            sp.dma_start(w_raw[:, :, DK0:2 * DK0], d["L0_xattn_W_v"].rearrange("(c p) n -> p c n", p=P)).then_inc(w_in, 16)
            sp.dma_start(w_raw[:, :, 2 * DK0:], d["L1_xattn_w_kv"].rearrange("(c p) n -> p c n", p=P)).then_inc(w_in, 16)
            sp.dma_start(st.head_mask0[:, :], d["head_mask0"]).then_inc(const_in, 16)
            sp.dma_start(st.head_mask1[:, :], d["head_mask1"]).then_inc(const_in, 16)

            def load_x(g):
                sp.dma_start(st.x[:, bass.ds(g * G, G), :, :].rearrange("p b q e -> p (b q) e"),
                             d["x"][bass.ds(g * G, G)].rearrange("b (q p) e -> p (b q) e", p=P)).then_inc(x_in, 16)

            load_x(0)
            with sp.Fori(1, B // G) as g:
                sp.wait_ge(ctxT_psum, g * DC)
                sp.dma_start(ctx_in[:, :, :], d["ctx"][bass.ds(g * G, G)].rearrange("b k e -> k b e")).then_inc(ctx_read, 16)
                load_x(g)
            load_raw(sp, d, st, ("L0_xattn_W_q", "L0_xattn_W_o"), raw_in)
            sp.wait_ge(raw_in, 32)
            sp.wait_ge(x_in, 16 * B // G)
            sp.wait_ge(const_in, 48)

        @block.gpsimd
        def _(pool):
            poolt = Ticking(pool, m.sem("pool_ticks"))
            pool.memset(st.minus_half[:, :], -0.5).then_inc(half_ready, 1)
            wait_apart(poolt, half_ready, 1)

        @block.tensor
        def _(pe):
            pe.wait_ge(const_in, 48)

            def group(g):
                pe.wait_ge(ctx_read, g * 16 + 16)
                for c in range(DC):
                    at_least(pe, ctxT_lo, g * DC + c - DC + 1)
                    for b in range(G):
                        last = nc.tensor.transpose(ctxT_ps[c][:, b * SK:(b + 1) * SK],
                                                   ctx_in[0:SK, b, c * P:(c + 1) * P], st.ident[0:SK, 0:SK])
                    last.then_inc(ctxT_psum, 1)
                pe.wait_ge(ctxT_lo, g * DC + DC)
                for j in range(3):
                    if j == 0:
                        pe.wait_ge(wk_ready, 1)
                    at_least(pe, key_done, g * 3 + j - 2)
                    for n, (c, (a, b)) in enumerate((c, ab) for c in range(DC) for ab in PASSES):
                        last = nc.tensor.matmul(key_ps[j][:, 0:GK], wk[a][:, c, j * P:(j + 1) * P],
                                                ctxT[b][:, c, :], start=n == 0, stop=n == 5)
                    last.then_inc(key_psum, 1)
                for k in range(G):
                    if k == 0:
                        pe.wait_ge(wv_ready, 1)
                    at_least(pe, val_done, g * G + k - 1)
                    for n, (c, (a, b)) in enumerate((c, ab) for c in range(DC) for ab in PASSES):
                        last = nc.tensor.matmul(val_ps[k % 2][0:SK, 0:VC], ctxT[a][:, c, k * SK:(k + 1) * SK],
                                                wv[b][:, c, :], start=n == 0, stop=n == 5)
                    last.then_inc(val_psum, 1)

            group(0)
            with pe.Fori(1, B // G) as g:
                group(g)

        @block.scalar
        def _(act):
            act.wait_ge(w_in, 48)
            for t, (out, lo, hi) in enumerate(((wk[0][:, :, 0:DK0], 0, DK0), (wk[0][:, :, DK0:P], 0, DK0),
                                               (wk[0][:, :, P:], 2 * DK0, 2 * DK0 + D),
                                               (wv[0][:, :, 0:DK0], DK0, 2 * DK0),
                                               (wv[0][:, :, DK0:], 2 * DK0 + D, 2 * DK0 + 2 * D))):
                nc.scalar.copy(out, w_raw[:, :, lo:hi]).then_inc(whi, 1)

            def group(g):
                for c in range(DC):
                    act.wait_ge(ctxT_psum, g * DC + c + 1)
                    at_least(act, val_psum, g * G)
                    nc.scalar.copy(ctxT[0][:, c, :], ctxT_ps[c][:, 0:GK]).then_inc(ctxT_hi, 1)
                for k in range(G):
                    act.wait_ge(val_psum, g * G + k + 1)
                    nc.scalar.copy(st.val0[0:SK, bass.ds(g * G + k, 1), :], val_ps[k % 2][0:SK, 0:DK0].unsqueeze(1))
                    nc.scalar.copy(st.val1[0:SK, bass.ds(g * G + k, 1), :],
                                   val_ps[k % 2][0:SK, DK0:VC].unsqueeze(1)).then_inc(val_done, 1)

            group(0)
            with act.Fori(1, B // G) as g:
                group(g)

        @block.vector
        def _(dve):
            for t, (i, a, b, lo, hi) in enumerate(((wk, 0, DK0, 0, DK0), (wk, DK0, P, 0, DK0),
                                                   (wk, P, P + D, 2 * DK0, 2 * DK0 + D),
                                                   (wv, 0, DK0, DK0, 2 * DK0),
                                                   (wv, DK0, VC, 2 * DK0 + D, 2 * DK0 + 2 * D))):
                dve.wait_ge(whi, t + 1)
                op = nc.vector.tensor_tensor(i[1][:, :, a:b], w_raw[:, :, lo:hi], fp32_of(i[0][:, :, a:b]), ALU.subtract)
                if t == 2:
                    op.then_inc(wk_ready, 1)
                if t == 4:
                    op.then_inc(wv_ready, 1)

            def group(g):
                for c in range(DC):
                    dve.wait_ge(ctxT_hi, g * DC + c + 1)
                    at_least(dve, val_psum, g * G)
                    nc.vector.tensor_tensor(ctxT[1][:, c, :], ctxT_ps[c][:, 0:GK], fp32_of(ctxT[0][:, c, :]),
                                            ALU.subtract).then_inc(ctxT_lo, 1)
                for j in range(3):
                    dve.wait_ge(key_psum, g * 3 + j + 1)
                    keys = key_ps[j][:, 0:GK].rearrange("p (b k) -> p b k", b=G)
                    out = st.key0[:, bass.ds(g * G, G), :] if j == 0 else st.key1[:, j - 1, bass.ds(g * G, G), :]
                    nc.vector.tensor_copy(out, keys).then_inc(key_done, 1)

            group(0)
            with dve.Fori(1, B // G) as g:
                group(g)


def x_rows(st, b, q):
    return st.x[:, bass.ds(b, 1), q, :].rearrange("p b e -> p (b e)")


class LayerNorm:

    def __init__(self, nc, m, st):
        self.nc, self.st = nc, st
        self.xn = m.sb("xn", [P, NC, D])
        self.stats = m.sb("stats", [P, NC, 6])
        self.mean_var = m.sb("mean_var", [P, NC, 2])
        self.var_eps = m.sb("var_eps", [P, NC])
        self.rstd = m.sb("rstd", [P, NC])
        self.ticks = m.sem("ln_pool_ticks"), m.sem("ln_dve_ticks")
        self.stats_step, self.stats_ready = m.sem("stats_step"), m.sem("stats_ready")
        self.var_ready, self.rstd_ready, self.ready = m.sem("var_ready"), m.sem("rstd_ready"), m.sem("ln_ready")

    def statistics(self, dve, f):
        at_least(dve, self.ready, NC * f)
        for q in range(NC):
            self.nc.vector.bn_stats(self.stats[:, q, :], x_rows(self.st, f, q)).then_inc(self.stats_step, 1)
        for q in range(NC):
            wait_apart(Ticking(dve, self.ticks[1]), self.stats_step, NC * f + q + 1)
            self.nc.vector.bn_aggr(self.mean_var[:, q, :], self.stats[:, q, :]).then_inc(self.stats_ready, 1)

    def inverse_deviation(self, pool, f):
        poolt = Ticking(pool, self.ticks[0])
        wait_apart(poolt, self.stats_ready, NC * f + NC)
        wait_apart(poolt, self.ready, NC * f)
        self.nc.gpsimd.tensor_scalar(self.var_eps[:, :], self.mean_var[:, :, 1], LN_EPS, None,
                                     ALU.add).then_inc(self.var_ready, 1)
        wait_apart(poolt, self.var_ready, f + 1)
        self.nc.gpsimd.tensor_tensor(self.rstd[:, :], self.var_eps[:, :], self.st.minus_half[:, 0:NC],
                                     ALU.pow).then_inc(self.rstd_ready, 1)

    def normalise(self, dve, f, read, reads):
        dve.wait_ge(self.rstd_ready, f + 1)
        at_least(dve, read, reads * f)
        for q in range(NC):
            self.nc.vector.tensor_scalar(self.xn[:, q, :], x_rows(self.st, f, q), self.mean_var[:, q, 0:1],
                                         self.rstd[:, q:q + 1], ALU.subtract, ALU.mult).then_inc(self.ready, 1)


def attention(nc, d, st, index):
    with ExitStack() as stack:
        m = Memory(nc, stack, f"att{index}")
        L0 = index == 0
        dk = DK0 if L0 else DK1
        QW = H * dk
        CH = QW // P
        PC = HP // CH
        HC = 2 * PC
        scale = dk ** -0.5
        wq = m.split("wq", [P, DC, QW])
        wo = m.split("wo", [P, CH, D])
        key, val = (st.key0, st.val0) if L0 else (st.key1, st.val1)
        head_mask = st.head_mask0 if L0 else st.head_mask1
        step_of_query = {c - 1: c for c in range(1, CH)}
        LN_STEP = 1
        RING = 4
        KC = 1 if L0 else CH
        KH = 2 if L0 else HC

        ln = LayerNorm(nc, m, st)
        xT = m.split("xT", [P, DC, N])
        qT = [m.sb(f"qT{i}", [P, N]) for i in range(2)]
        keys = m.sb("keys", [P, KC, KH, SK])
        vals = m.split("vals", [P, (2 if L0 else H) * P + HC * dk])
        mx = [m.sb(f"mx{i}", [P, 2 * NC]) for i in range(2)]
        ex = [m.sb(f"ex{i}", [P, 2 * NC, SK]) for i in range(RING)]
        rsum = [m.sb(f"rsum{i}", [P, 2 * NC]) for i in range(RING)]
        rinv = [m.sb(f"rinv{i}", [P, 2 * NC]) for i in range(RING)]
        PW = (H - 1) * SK + P
        prob = m.sb("prob", [P, NC, PW])
        pT = [m.split(f"pT{i}", [P, 2 * N]) for i in range(2)]
        oT = m.split("oT", [P, CH, N])
        if L0:
            ident16 = m.sb("ident16", [P, P], BF16)
            causal_raw = m.sb("causal_raw", [P, PAIR])
            causal16 = m.sb("causal16", [P, PAIR], BF16)
        else:
            pos_raw = m.sb("pos_raw", [P, N])
            pos16 = m.sb("pos16", [P, N], BF16)
            w_rel = m.sb("w_rel", [H, 1])
            neg_k = m.sb("neg_k", [H, SK])
            slope = m.sb("slope", [H, 2, SK])
            part = m.sb("part", [H, 2, SK])
            part16 = m.sb("part16", [H, 3, 2, SK], BF16)
            bias16 = m.sb("bias16", [P, H, SK], BF16)

        q_bank = [m.ps(f"q_bank{i}") for i in range(2)]
        s_bank = [m.ps(f"s_bank{i}") for i in range(2)]
        t_bank = [m.ps(f"t_bank{i}") for i in range(2)]
        o_bank = [m.ps(f"o_bank{i}") for i in range(2)]

        w_hi, w_ready, raw_in = m.sem("w_hi"), m.sem("w_ready"), m.sem("raw_in")
        bias_in, vals_zero = m.sem("bias_in"), m.sem("vals_zero")
        c_in, c_ready, zeroed, c_step = m.sem("c_in"), m.sem("c_ready"), m.sem("zeroed"), m.sem("c_step")
        xt_psum, xt_hi, xt_lo = m.sem("xt_psum"), m.sem("xt_hi"), m.sem("xt_lo")
        q_psum, q_ready = m.sem("q_psum"), m.sem("q_ready")
        keys_ready, vals_hi, vals_ready = m.sem("keys_ready"), m.sem("vals_hi"), m.sem("vals_ready")
        s_psum, mx_ready, shifted, ex_ready = m.sem("s_psum"), m.sem("mx_ready"), m.sem("shifted"), m.sem("ex_ready")
        sum_ready, scores_read = m.sem("sum_ready"), ex_ready
        inv_ready, p_ready = m.sem("inv_ready"), m.sem("p_ready")
        t_psum, pt_hi, pt_lo = m.sem("t_psum"), m.sem("pt_hi"), m.sem("pt_lo")
        pv_done, ot_hi, ot_lo = m.sem("pv_done"), m.sem("ot_hi"), m.sem("ot_lo")
        proj_psum, x_done = m.sem("proj_psum"), m.sem("x_done")
        stack.callback(m.end_phase)
        block = stack.enter_context(nc.Block())

        def loop(eng, body):
            body(0, True, False, True)
            body(1, True, True, True)
            with eng.Fori(2, B - 1) as f:
                body(f, True, True, True)
            body(B - 1, True, True, False)
            body(B, False, True, False)

        def raw_weights(i):
            rows = (DC, CH)[i]
            return st.raw[:, i * DC * QW:(i + 1) * DC * QW].rearrange("p (c n) -> p c n", c=rows)

        @block.sync
        def _(sp):
            if L0:
                sp.dma_start(causal_raw[:, :], d["causal"]).then_inc(c_in, 16)
            else:
                sp.dma_start(w_rel[:, :], d["L1_xattn_w_rel"].rearrange("a h -> h a")).then_inc(c_in, 16)
                sp.dma_start(neg_k[:, :], d["neg_k"]).then_inc(c_in, 16)
                sp.dma_start(pos_raw[:, :], d["positions"]).then_inc(c_in, 16)
                sp.wait_ge(zeroed, 1)
                sp.wait_ge(c_step, 8)
                for i in range(3):
                    for r in range(2):
                        sp.dma_start(bias16[3 * r + i:3 * r + i + 1, :, :], part16[:, i, r, :]).then_inc(bias_in, 16)
                sp.wait_ge(bias_in, 96)
            if L0:
                sp.wait_ge(w_ready, 2)
                load_raw(sp, d, st, ("L0_ffn_w1", "L0_ffn_w2"), raw_in)
                sp.wait_ge(raw_in, 32)

        @block.tensor
        def _(pe):
            def transpose_x(f):
                for c in range(DC):
                    pe.wait_ge(ln.ready, NC * f + NC)
                    if not isinstance(f, int) or f > 0:
                        pe.wait_ge(q_ready, CH * f - DC + c + 1)
                    for q in range(NC):
                        last = nc.tensor.transpose(q_bank[c][:, q * P:(q + 1) * P],
                                                   ln.xn[:, q, c * P:(c + 1) * P], st.ident[:, :])
                    last.then_inc(xt_psum, 1)

            def queries(f, c):
                pe.wait_ge(xt_lo, DC * f + DC)
                if c == 1:
                    at_least(pe, x_done, NC * (f - 1))
                if c >= 2:
                    pe.wait_ge(q_ready, CH * f + c - 1)
                for n, (k, (a, b)) in enumerate((k, ab) for k in range(DC) for ab in PASSES):
                    last = nc.tensor.matmul(q_bank[c % 2][:, 0:N], wq[a][:, k, c * P:(c + 1) * P],
                                            xT[b][:, k, :], start=n == 0, stop=n == 5)
                last.then_inc(q_psum, 1)

            def scores(f, t):
                c = t // PC
                pe.wait_ge(q_ready, CH * f + c + 1)
                if t % (HP // KC) == 0:
                    pe.wait_ge(keys_ready, KC * f + t * KC // HP + 1)
                at_least(pe, scores_read, HP * f + t - 1)
                if t == 0:
                    at_least(pe, x_done, NC * (f - 2) + 1)
                kc, h0 = (0, 0) if L0 else (c, 2 * (t % PC))
                for q in range(NC):
                    out = s_bank[t % 2][:, q * PAIR:(q + 1) * PAIR]
                    first = True
                    if L0 and q == 0:
                        nc.tensor.matmul(out, ident16[:, :], causal16[:, :], start=True, stop=False)
                        first = False
                    if not L0:
                        nc.tensor.matmul(out, pos16[:, q * P:(q + 1) * P], bias16[:, 2 * t:2 * t + 2, :], start=True, stop=False)
                        first = False
                    last = nc.tensor.matmul(out, qT[c % 2][:, q * P:(q + 1) * P], keys[:, kc, h0:h0 + 2, :],
                                            start=first, stop=True)
                last.then_inc(s_psum, 1)

            def transpose_p(g, t):
                pe.wait_ge(p_ready, HP * g + min(t + 2, HP))
                at_least(pe, pt_lo, HP * g + t - 1)
                for h in range(2):
                    for q in range(NC):
                        last = nc.tensor.transpose(t_bank[t % 2][:, h * N + q * P:h * N + (q + 1) * P],
                                                   prob[:, q, (2 * t + h) * SK:(2 * t + h) * SK + P], st.ident[:, :])
                last.then_inc(t_psum, 1)

            def weigh_values(g, t):
                j = t // PC
                pe.wait_ge(pt_lo, HP * g + t + 1)
                if t % (HP // KC) == 0:
                    pe.wait_ge(vals_ready, KC * g + t * KC // HP + 1)
                if t % PC == 0:
                    at_least(pe, ot_lo, CH * g + j - 1)
                for h in range(2):
                    v = h if L0 else 2 * t + h
                    for n, (a, b) in enumerate(PASSES):
                        last = nc.tensor.matmul(o_bank[j % 2][:, 0:N], vals[a][:, v * P:(v + 1) * P], pT[t % 2][b][:, h * N:(h + 1) * N],
                                                start=t % PC == 0 and h == 0 and n == 0,
                                                stop=t % PC == PC - 1 and h == 1 and n == 2)
                last.then_inc(pv_done, 1)

            def project(g, q, chunks):
                if isinstance(g, int) and g == 0:
                    pe.wait_ge(w_ready, 2)
                for j in chunks:
                    pe.wait_ge(ot_lo, CH * g + j + 1)
                    for n, (a, b) in enumerate(PASSES):
                        last = nc.tensor.matmul((s_bank[0], q_bank[1])[q][:, 0:D], oT[a][:, j, q * P:(q + 1) * P],
                                                wo[b][:, j, :], start=j == 0 and n == 0, stop=j == CH - 1 and n == 2)
                    if j == CH - 1:
                        last.then_inc(proj_psum, 1)

            def batch(f, front, back, following):
                g = f - 1
                for t in range(HP):
                    if front and t in step_of_query and t > 0:
                        queries(f, step_of_query[t])
                    if back:
                        transpose_p(g, t)
                    if front:
                        scores(f, t)
                    if front and t in step_of_query and t == 0:
                        queries(f, step_of_query[t])
                    if back and t >= 1:
                        weigh_values(g, t - 1)
                if following:
                    transpose_x(f + 1)
                if back:
                    pe.wait_ge(scores_read, HP * f + HP - 1 if front else HP * B)
                    if not front:
                        pe.wait_ge(x_done, NC * g)
                    project(g, 0, range(CH - 2))
                    weigh_values(g, HP - 1)
                    if following:
                        pe.wait_ge(xt_lo, DC * (f + 1) + DC)
                    elif front:
                        pe.wait_ge(q_ready, CH * B)
                    project(g, 1, range(CH - 2))
                    for q in range(NC):
                        project(g, q, (CH - 2,))
                if following:
                    queries(f + 1, 0)
                if back:
                    for q in range(NC):
                        project(g, q, (CH - 1,))

            transpose_x(0)
            pe.wait_ge(w_ready, 1)
            queries(0, 0)
            pe.wait_ge(c_ready, 1)
            if not L0:
                pe.wait_ge(bias_in, 96)
            loop(pe, batch)

        @block.scalar
        def _(act):
            nc.scalar.copy(wq[0][:, :, :], raw_weights(0)).then_inc(w_hi, 1)

            def transposed_x(f):
                for c in range(DC):
                    act.wait_ge(xt_psum, DC * f + c + 1)
                    nc.scalar.copy(xT[0][:, c, :], q_bank[c][:, 0:N]).then_inc(xt_hi, 1)

            def batch(f, front, back, following):
                g = f - 1
                for t in range(HP + 1):
                    if front and t in step_of_query and t > 0:
                        scale_queries(f, step_of_query[t])
                    if back and t < HP:
                        act.wait_ge(t_psum, HP * g + t + 1)
                        at_least(act, pv_done, HP * g + t - 1)
                        nc.scalar.copy(pT[t % 2][0][:, :], t_bank[t % 2][:, :]).then_inc(pt_hi, 1)
                    if front and t in step_of_query and t == 0:
                        scale_queries(f, step_of_query[t])
                    if following and t == HP:
                        transposed_x(f + 1)
                    if front and t >= 1:
                        exponentials(f, t - 1)
                    if back and t >= 2 and (t - 1) % PC == 0:
                        copy_heads(g, (t - 1) // PC - 1)
                if back:
                    copy_heads(g, CH - 1)
                if following:
                    scale_queries(f + 1, 0)

            def exponentials(f, t):
                act.wait_ge(mx_ready, HP * f + t + 1)
                at_least(act, p_ready, HP * f + t - RING + 1)
                for r in range(2 * NC):
                    last = nc.scalar.activation(ex[t % RING][:, r, :], s_bank[t % 2][:, r * SK:(r + 1) * SK], ACT.Exp,
                                                bias=mx[t % 2][:, r:r + 1])
                last.then_inc(ex_ready, 1)

            def scale_queries(f, c):
                act.wait_ge(q_psum, CH * f + c + 1)
                at_least(act, s_psum, HP * f + (c - 1) * PC)
                nc.scalar.mul(qT[c % 2][:, :], q_bank[c % 2][:, 0:N], scale).then_inc(q_ready, 1)

            def copy_heads(g, j):
                act.wait_ge(pv_done, HP * g + (j + 1) * PC)
                at_least(act, proj_psum, NC * g)
                nc.scalar.copy(oT[0][:, j, :], o_bank[j % 2][:, 0:N]).then_inc(ot_hi, 1)

            transposed_x(0)
            nc.scalar.copy(wo[0][:, :, :], raw_weights(1)).then_inc(w_hi, 1)
            scale_queries(0, 0)
            loop(act, batch)

        @block.vector
        def _(dve):
            def transposed_x(f):
                for c in range(DC):
                    dve.wait_ge(xt_hi, DC * f + c + 1)
                    nc.vector.tensor_tensor(xT[1][:, c, :], q_bank[c][:, 0:N], fp32_of(xT[0][:, c, :]),
                                            ALU.subtract).then_inc(xt_lo, 1)

            def row_scores(t):
                return s_bank[t % 2][:, 0:NC * PAIR].rearrange("p (r k) -> p r k", k=SK)

            def find_maxima(f, t):
                dve.wait_ge(s_psum, HP * f + t + 1)
                at_least(dve, scores_read, HP * f + t - 1)
                nc.vector.tensor_reduce(mx[t % 2][:, :], row_scores(t), AX, ALU.max, negate=True).then_inc(mx_ready, 1)

            def shift(f, t):
                dve.wait_ge(mx_ready, HP * f + t + 1)
                at_least(dve, p_ready, HP * f + t - RING + 1)
                nc.vector.tensor_tensor(ex[t % RING][:, :, :], row_scores(t),
                                        mx[t % 2][:, :].unsqueeze(2).to_broadcast([P, 2 * NC, SK]),
                                        ALU.subtract).then_inc(shifted, 1)

            def add_up(f, t):
                dve.wait_ge(ex_ready, HP * f + t + 1)
                nc.vector.tensor_reduce(rsum[t % RING][:, :], ex[t % RING][:, :, :], AX, ALU.add).then_inc(sum_ready, 1)

            def invert(f, t):
                dve.wait_ge(sum_ready, HP * f + t + 1)
                at_least(dve, p_ready, HP * f + t - RING + 1)
                nc.vector.reciprocal(rinv[t % RING][:, :], rsum[t % RING][:, :]).then_inc(inv_ready, 1)

            def split_heads(g, j):
                dve.wait_ge(ot_hi, CH * g + j + 1)
                nc.vector.tensor_tensor(oT[1][:, j, :], o_bank[j % 2][:, 0:N], fp32_of(oT[0][:, j, :]),
                                        ALU.subtract).then_inc(ot_lo, 1)

            def batch(f, front, back, following):
                g = f - 1
                for t in range(HP + 2):
                    if front and 1 <= t <= HP:
                        find_maxima(f, t - 1)
                    if following and t == HP:
                        transposed_x(f + 1)
                    if front and t >= 2:
                        add_up(f, t - 2)
                    if front and t >= 2:
                        invert(f, t - 2)
                    if following and t == LN_STEP:
                        ln.statistics(dve, f + 1)
                    if back and t < HP:
                        dve.wait_ge(pt_hi, HP * g + t + 1)
                        nc.vector.tensor_tensor(pT[t % 2][1][:, :], t_bank[t % 2][:, :], fp32_of(pT[t % 2][0][:, :]),
                                                ALU.subtract).then_inc(pt_lo, 1)
                    if back and 2 <= t <= HP and (t - 1) % PC == 0:
                        split_heads(g, (t - 1) // PC - 1)
                    if following and t == LN_STEP + 2:
                        ln.normalise(dve, f + 1, xt_psum, DC)
                if back:
                    split_heads(g, CH - 1)
                    for q in range(NC):
                        dve.wait_ge(proj_psum, NC * g + q + 1)
                        nc.vector.tensor_tensor(x_rows(st, g, q), (s_bank[0], q_bank[1])[q][:, 0:D], x_rows(st, g, q), ALU.add).then_inc(x_done, 1)

            def split_weights(i):
                w = (wq, wo)[i]
                dve.wait_ge(w_hi, i + 1)
                nc.vector.tensor_tensor(w[1][:, :, :], raw_weights(i), fp32_of(w[0][:, :, :]), ALU.subtract).then_inc(w_ready, 1)

            def constants_of_the_scores():
                if L0:
                    dve.wait_ge(c_in, 16)
                    nc.vector.tensor_copy(ident16[:, :], st.ident[:, :])
                    nc.vector.tensor_copy(causal16[:, :], causal_raw[:, :]).then_inc(c_ready, 1)
                    return
                dve.wait_ge(c_in, 16 * 3)
                nc.vector.tensor_copy(slope[:, 0, :], w_rel[:, :].to_broadcast([H, SK]))
                nc.vector.tensor_tensor(slope[:, 1, :], w_rel[:, :].to_broadcast([H, SK]), neg_k[:, :], ALU.mult).then_inc(c_step, 1)
                nc.vector.tensor_copy(pos16[:, :], pos_raw[:, :]).then_inc(c_ready, 1)
                for i in range(3):
                    dve.wait_ge(c_step, 3 * i + 1)
                    nc.vector.tensor_copy(part16[:, i, :, :], slope[:, :, :]).then_inc(c_step, 1)
                    if i < 2:
                        dve.wait_ge(c_step, 3 * i + 2)
                        nc.vector.tensor_copy(part[:, :, :], part16[:, i, :, :]).then_inc(c_step, 1)
                        dve.wait_ge(c_step, 3 * i + 3)
                        nc.vector.tensor_tensor(slope[:, :, :], slope[:, :, :], part[:, :, :], ALU.subtract).then_inc(c_step, 1)

            ln.statistics(dve, 0)
            if not L0:
                constants_of_the_scores()
            ln.normalise(dve, 0, xt_psum, DC)
            split_weights(0)
            transposed_x(0)
            if L0:
                constants_of_the_scores()
            for v in vals:
                nc.vector.memset(fp32_of(v[:, :]), 0.0).then_inc(vals_zero, 1)
            split_weights(1)
            loop(dve, batch)

        @block.gpsimd
        def _(pool):
            poolt = Ticking(pool, m.sem("pool_ticks"))
            ln.inverse_deviation(pool, 0)
            if not L0:
                pool.memset(bias16[:, :, :], 0.0).then_inc(zeroed, 1)

            def lay_out_keys(f, c):
                wait_apart(poolt, s_psum, HP * (f - 1) + (c + 1) * HP // KC)
                mask = head_mask[:, :].unsqueeze(2).to_broadcast([P, KH, SK])
                k = key[:, bass.ds(f, 1), :] if L0 else key[:, c, bass.ds(f, 1), :]
                nc.gpsimd.tensor_tensor(keys[:, c, :, :], k.to_broadcast([P, KH, SK]), mask, ALU.mult).then_inc(keys_ready, 1)

            def lay_out_values(g, c):
                if isinstance(g, int) and g == 0:
                    wait_apart(poolt, vals_zero, 2)
                wait_apart(poolt, pv_done, HP * (g - 1) + (c + 1) * HP // KC)
                if L0:
                    v = val[0:SK, bass.ds(g, 1), :].to_broadcast([SK, HC, dk])
                else:
                    v = val[0:SK, bass.ds(g, 1), c * P:(c + 1) * P].rearrange("p b (h e) -> p (b h) e", e=dk)
                hi, lo = (diagonal(tile, c) for tile in vals)
                nc.gpsimd.tensor_copy(hi, v).then_inc(vals_hi, 1)
                wait_apart(poolt, vals_hi, KC * g + c + 1)
                nc.gpsimd.tensor_tensor(lo, v, fp32_of(hi), ALU.subtract).then_inc(vals_ready, 1)

            def diagonal(v, c):
                return v[0:SK, c * HC * P:c * HC * P + HC * (P + dk)].rearrange("p (h n) -> p h n", n=P + dk)[:, :, 0:dk]

            def batch(f, front, back, following):
                g = f - 1
                if back:
                    lay_out_values(g, KC - 1)
                if front and not (isinstance(f, int) and f == 0):
                    lay_out_keys(f, KC - 1)
                if front:
                    for t in range(HP):
                        if following and t == max(LN_STEP - 1, 0):
                            ln.inverse_deviation(pool, f + 1)
                        wait_apart(poolt, inv_ready, HP * f + t + 1)
                        if back:
                            wait_apart(poolt, t_psum, HP * g + t + 1)
                        e = ex[t % RING][:, :, :].rearrange("p (q h) k -> p q h k", q=NC)
                        w = rinv[t % RING][:, :].rearrange("p (q h) -> p q h", q=NC).unsqueeze(3).to_broadcast([P, NC, 2, SK])
                        out = prob[:, :, t * PAIR:(t + 1) * PAIR].rearrange("p q (h k) -> p q h k", h=2)
                        nc.gpsimd.tensor_tensor(out, e, w, ALU.mult).then_inc(p_ready, 1)
                        if KC > 1 and t == HP // 2:
                            lay_out_values(f, 0)
                            if following:
                                lay_out_keys(f + 1, 0)

            for c in range(KC):
                lay_out_keys(0, c)
            pool.memset(prob[:, :, H * SK:], 0.0)
            loop(pool, batch)


def ffn(nc, d, st):
    LAG = 3
    with ExitStack() as stack:
        m = Memory(nc, stack, "ffn")
        w1 = m.split("w1", [P, DC, FC, P])
        w2 = m.split("w2", [P, FC, D])
        b1 = m.sb("b1", [P, FC])
        b2 = m.sb("b2", [P, D])
        ln = LayerNorm(nc, m, st)
        xT = m.split("xT", [P, DC, N])
        xb = m.sb("xb", [P, NC, D])
        RING = 3
        hid = [m.sb(f"hid{i}", [P, N]) for i in range(2)]
        hT = [m.split(f"hT{i}", [P, N]) for i in range(RING + 1)]
        xt_bank = [m.ps(f"xt_bank{c}") for c in range(DC)]
        h_bank = [m.ps(f"h_bank{i}") for i in range(4)]
        o_bank = [m.ps(f"o_bank{i}") for i in range(NC)]
        raw_in, w_hi, w_ready, b_in = m.sem("raw_in"), m.sem("w_hi"), m.sem("w_ready"), m.sem("b_in")
        xt_psum, xt_hi, xt_lo = m.sem("xt_psum"), m.sem("xt_hi"), m.sem("xt_lo")
        h_psum, hid_ready, hid_hi, hid_lo = m.sem("h_psum"), m.sem("hid_ready"), m.sem("hid_hi"), m.sem("hid_lo")
        down_done, x_done, xb_ready = m.sem("down_done"), m.sem("x_done"), m.sem("xb_ready")
        stack.callback(m.end_phase)
        block = stack.enter_context(nc.Block())

        def raw_part(i, k):
            raw = st.raw[:, (2 * i + k) * FF:(2 * i + k + 1) * FF]
            return raw.rearrange("p (j t) -> p t j", t=FC) if i == 0 else raw.rearrange("p (c n) -> p c n", n=D)

        def part_of(w, i, k):
            return w[:, k, :, :] if i == 0 else w[:, k * FC // 2:(k + 1) * FC // 2, :]

        def loop(eng, body):
            body(0, True)
            with eng.Fori(1, B - 1) as f:
                body(f, True)
            body(B - 1, False)

        @block.sync
        def _(sp):
            sp.dma_start(b1[:, :], d["L0_ffn_b1"].rearrange("(p c) -> p c", p=P)).then_inc(b_in, 16)
            sp.dma_start(b2[:, :], d["L0_ffn_b2"].rearrange("(a n) -> a n", a=1).broadcast_to([P, D])).then_inc(b_in, 16)
            sp.wait_ge(w_ready, 2 * DC)
            load_raw(sp, d, st, ("L1_xattn_w_q", "L1_xattn_w_proj", "L1_ffn_mu"), raw_in)
            sp.wait_ge(raw_in, 48)

        @block.tensor
        def _(pe):
            def transpose_x(f):
                pe.wait_ge(ln.ready, NC * f + NC)
                for c in range(DC):
                    at_least(pe, xt_lo, DC * (f - 1) + c + 1)
                    for q in range(NC):
                        last = nc.tensor.transpose(xt_bank[c][:, q * P:(q + 1) * P],
                                                   ln.xn[:, q, c * P:(c + 1) * P], st.ident[:, :])
                    last.then_inc(xt_psum, 1)

            def up(f, t):
                pe.wait_ge(xt_lo, DC * f + DC)
                at_least(pe, hid_ready, FC * f + t - 3)
                for n, (k, (a, b)) in enumerate((k, ab) for k in range(DC) for ab in PASSES):
                    last = nc.tensor.matmul(h_bank[t % 4][:, 0:N], w1[a][:, k, t, :],
                                            xT[b][:, k, :], start=n == 0, stop=n == 5)
                last.then_inc(h_psum, 1)

            def down(f, t):
                pe.wait_ge(hid_lo, FC * f + t + 1)
                if t == 0:
                    at_least(pe, x_done, NC * f)
                    if isinstance(f, int) and f == 0:
                        pe.wait_ge(w_ready, 2 * DC)
                h = hT[t % (RING + 1)]
                for q in range(NC):
                    for n, (a, b) in enumerate(PASSES):
                        last = nc.tensor.matmul(o_bank[q][:, 0:D], h[a][:, q * P:(q + 1) * P], w2[b][:, t, :],
                                                start=t == 0 and n == 0, stop=t == FC - 1 and n == 2)
                last.then_inc(down_done, 1)

            def batch(f, following):
                for t in range(FC):
                    up(f, t)
                    if following and t == FC - 1:
                        transpose_x(f + 1)
                    if t >= LAG:
                        down(f, t - LAG)
                for t in range(FC - LAG, FC):
                    down(f, t)

            transpose_x(0)
            pe.wait_ge(w_ready, DC)
            loop(pe, batch)

        @block.scalar
        def _(act):
            def transposed_x(f):
                for c in range(DC):
                    act.wait_ge(xt_psum, DC * f + c + 1)
                    nc.scalar.copy(xT[0][:, c, :], xt_bank[c][:, 0:N]).then_inc(xt_hi, 1)

            def batch(f, following):
                for t in range(FC):
                    act.wait_ge(h_psum, FC * f + t + 1)
                    at_least(act, hid_lo, FC * f + t - 1)
                    nc.scalar.activation(hid[t % 2][:, :], h_bank[t % 4][:, 0:N], ACT.Gelu,
                                         bias=b1[:, t:t + 1]).then_inc(hid_ready, 1)
                if following:
                    transposed_x(f + 1)

            for i, w in enumerate((w1, w2)):
                for k in range(DC):
                    nc.scalar.copy(part_of(w[0], i, k), raw_part(i, k)).then_inc(w_hi, 1)
                if i == 0:
                    transposed_x(0)
            act.wait_ge(b_in, 32)
            loop(act, batch)

        @block.vector
        def _(dve):
            def transposed_x(f):
                for c in range(DC):
                    dve.wait_ge(xt_hi, DC * f + c + 1)
                    nc.vector.tensor_tensor(xT[1][:, c, :], xt_bank[c][:, 0:N], fp32_of(xT[0][:, c, :]),
                                            ALU.subtract).then_inc(xt_lo, 1)

            def batch(f, following):
                for t in range(FC):
                    n = FC * f + t
                    h = hT[t % (RING + 1)]
                    dve.wait_ge(hid_ready, n + 1)
                    at_least(dve, down_done, n - RING)
                    nc.vector.tensor_copy(h[0][:, :], hid[t % 2][:, :]).then_inc(hid_hi, 1)
                    if t == 3 and following:
                        ln.normalise(dve, f + 1, xt_psum, DC)
                    dve.wait_ge(hid_hi, n + 1)
                    nc.vector.tensor_tensor(h[1][:, :], hid[t % 2][:, :], fp32_of(h[0][:, :]), ALU.subtract).then_inc(hid_lo, 1)
                    if t == 1 and following:
                        ln.statistics(dve, f + 1)
                if following:
                    transposed_x(f + 1)
                dve.wait_ge(xb_ready, f + 1)
                dve.wait_ge(down_done, FC * f + FC)
                for q in range(NC):
                    nc.vector.tensor_tensor(x_rows(st, f, q), o_bank[q][:, 0:D], xb[:, q, :], ALU.add).then_inc(x_done, 1)

            ln.statistics(dve, 0)
            ln.normalise(dve, 0, xt_psum, DC)
            for i, w in enumerate((w1, w2)):
                for k in range(DC):
                    dve.wait_ge(w_hi, DC * i + k + 1)
                    nc.vector.tensor_tensor(part_of(w[1], i, k), raw_part(i, k), fp32_of(part_of(w[0], i, k)),
                                            ALU.subtract).then_inc(w_ready, 1)
                if i == 0:
                    transposed_x(0)
            loop(dve, batch)

        @block.gpsimd
        def _(pool):
            poolt = Ticking(pool, m.sem("pool_ticks"))
            def batch(f, following):
                if following:
                    ln.inverse_deviation(pool, f + 1)
                wait_apart(poolt, x_done, NC * f)
                nc.gpsimd.tensor_tensor(xb[:, :, :], st.x[:, bass.ds(f, 1), :, :].rearrange("p b q e -> p (b q) e"),
                                        b2[:, :].unsqueeze(1).to_broadcast([P, NC, D]), ALU.add).then_inc(xb_ready, 1)

            ln.inverse_deviation(pool, 0)
            wait_apart(poolt, b_in, 32)
            loop(pool, batch)


def batch_pairs(eng, body):
    body(0, 0, True, False, True)
    body(1, 1, True, True, True)
    body(2, 0, True, True, True)
    with eng.Fori(1, B // 2 - 1) as i:
        body(2 * i + 1, 1, True, True, True)
        body(2 * i + 2, 0, True, True, True)
    body(B - 1, 1, True, True, False)
    body(B, 0, False, True, False)


def batch_pairs_ahead(eng, body):
    body(0, 0, True, False, True, True, True)
    body(1, 1, True, True, True, True, True)
    body(2, 0, True, True, True, True, True)
    with eng.Fori(1, B // 2 - 2) as i:
        body(2 * i + 1, 1, True, True, True, True, True)
        body(2 * i + 2, 0, True, True, True, True, True)
    body(B - 3, 1, True, True, True, True, False)
    body(B - 2, 0, True, True, True, False, False)
    body(B - 1, 1, True, True, False, False, False)
    body(B, 0, False, True, False, False, False)


ES = E * S
EC = ES // P
NORM_EPS = 1e-12


def route(nc, d, st):
    with ExitStack() as stack:
        m = Memory(nc, stack, "route")
        gamma, beta = m.sb("gamma", [P, D]), m.sb("beta", [P, D])
        scale = m.sb("scale", [P, 1])
        mu_raw = st.raw[:, 2 * DC * D:2 * DC * D + DC * ES].rearrange("p (c n) -> p c n", c=DC)
        mu_sq = m.sb("mu_sq", [P, DC, ES])
        mu_sum, mu_norm, mu_max, mu_inv = (m.sb(n, [P, EC]) for n in ("mu_sum", "mu_norm", "mu_max", "mu_inv"))
        mu_diag, mu_unit = m.sb("mu_diag", [P, EC, P]), m.sb("mu_unit", [P, DC, ES])
        mu = m.split("mu", [P, DC, ES])
        ones = m.sb("ones", [P, P])
        half = m.sb("half", [P, NC])
        ln = LayerNorm(nc, m, st)
        xg = m.sb("xg", [P, NC, D])
        xa = [m.sb(f"xa{i}", [P, NC, D]) for i in range(2)]
        sq = m.sb("sq", [P, D])
        sumsq, length, length_min, inv_length = (m.sb(n, [P, NC]) for n in ("sumsq", "length", "length_min", "inv_length"))
        xu = m.sb("xu", [P, NC, D])
        xaS = [m.split(f"xaS{i}", [P, NC, D]) for i in range(2)]
        xT = [m.split(f"xT{i}", [P, DC, N]) for i in range(2)]
        top = [m.sb(f"top{k}", [P, 2]) for k in range(2)]
        ex = [m.sb(f"ex{k}", [P, 2, ES]) for k in range(2)]
        rsum = [m.sb(f"rsum{k}", [P, 2]) for k in range(2)]
        rinv = [m.sb(f"rinv{k}", [P, 2]) for k in range(2)]
        weight = [m.sb(f"weight{k}", [P, 2, ES]) for k in range(2)]
        disp = m.split("disp", [P, NC, ES])
        x_bank = [m.ps(f"x_bank{c}") for c in range(DC)]
        l_bank = [m.ps(f"l_bank{k}") for k in range(2)]
        t_bank = [m.ps(f"t_bank{k}") for k in range(2)]
        i_bank = m.ps("i_bank")

        in_ = m.sem("small_in")
        const_ready, mu_step, mu_psum, mu_ready = m.sem("const_ready"), m.sem("mu_step"), m.sem("mu_psum"), m.sem("mu_ready")
        mu_pow = m.sem("mu_pow")
        xg_ready, xa_ready, sq_step, sumsq_ready = m.sem("xg_ready"), m.sem("xa_ready"), m.sem("sq_step"), m.sem("sumsq_ready")
        len_ready, lmin_ready, inv_ready, xu_ready = m.sem("len_ready"), m.sem("lmin_ready"), m.sem("inv_ready"), m.sem("xu_ready")
        xas_hi, xas_ready = m.sem("xas_hi"), m.sem("xas_ready")
        xt_psum, xt_hi, xt_lo = m.sem("xt_psum"), m.sem("xt_hi"), m.sem("xt_lo")
        l_psum, top_ready, ex_ready = m.sem("l_psum"), m.sem("top_ready"), m.sem("ex_ready")
        rinv_ready, weight_ready = m.sem("rinv_ready"), m.sem("weight_ready")
        t_psum, comb_stored, disp_hi, disp_lo = m.sem("t_psum"), m.sem("comb_stored"), m.sem("disp_hi"), m.sem("disp_lo")
        i_psum, slots_stored = m.sem("i_psum"), m.sem("slots_stored")
        stack.callback(m.end_phase)
        block = stack.enter_context(nc.Block())

        @block.sync
        def _(sp):
            row = lambda name: d[name].rearrange("(a n) -> a n", a=1)
            sp.dma_start(gamma[:, :], row("L1_ffn_ln_gamma").broadcast_to([P, D])).then_inc(in_, 16)
            sp.dma_start(beta[:, :], row("L1_ffn_ln_beta").broadcast_to([P, D])).then_inc(in_, 16)
            sp.dma_start(scale[:, :], row("L1_ffn_scale").broadcast_to([P, 1])).then_inc(in_, 16)

        @block.tensor
        def _(pe):
            def transpose_x(f):
                pe.wait_ge(xu_ready, NC * f + NC)
                for c in range(DC):
                    at_least(pe, xt_lo, DC * (f - 1) + c + 1)
                    for q in range(NC):
                        last = nc.tensor.transpose(x_bank[c][:, q * P:(q + 1) * P],
                                                   xu[:, q, c * P:(c + 1) * P], st.ident[:, :])
                    last.then_inc(xt_psum, 1)

            def logits(f, i, k):
                pe.wait_ge(xt_lo, DC * f + DC)
                at_least(pe, ex_ready, 4 * (f - 1) + 2 * k + 2)
                rows, cols = ((mu, xT[i]), (xT[i], mu))[k]
                for r in range(2):
                    for n, (c, (a, b)) in enumerate((c, ab) for c in range(DC) for ab in PASSES):
                        last = nc.tensor.matmul(l_bank[k][:, r * ES:(r + 1) * ES], rows[a][:, c, r * P:(r + 1) * P],
                                                cols[b][:, c, :], start=n == 0, stop=n == 5)
                last.then_inc(l_psum, 1)

            def transpose_weights(g):
                for k in range(2):
                    pe.wait_ge(weight_ready, 4 * g + 2 * k + 2)
                    at_least(pe, (disp_lo, comb_stored)[k], g)
                    for r in range(2):
                        for j in range(2):
                            last = nc.tensor.transpose(t_bank[k][:, j * ES + r * P:j * ES + (r + 1) * P],
                                                       weight[k][:, r, j * P:(j + 1) * P], st.ident[:, :])
                    last.then_inc(t_psum, 1)

            def slot_inputs(g, i):
                pe.wait_ge(disp_lo, g + 1)
                pe.wait_ge(xas_ready, g + 1)
                at_least(pe, slots_stored, g)
                for c in range(DC):
                    for n, (q, (a, b)) in enumerate((q, ab) for q in range(NC) for ab in PASSES):
                        last = nc.tensor.matmul(i_bank[:, c * ES:(c + 1) * ES], xaS[i][a][:, q, c * P:(c + 1) * P],
                                                disp[b][:, q, :], start=n == 0, stop=n == 5)
                last.then_inc(i_psum, 1)

            def batch(f, i, front, back, following, later, latest):
                if front:
                    logits(f, i, 0)
                if back:
                    transpose_weights(f - 1)
                if front:
                    logits(f, i, 1)
                if following:
                    transpose_x(f + 1)
                if back:
                    slot_inputs(f - 1, 1 - i)

            pe.wait_ge(const_ready, 2)
            pe.wait_ge(mu_step, 1)
            for j in range(EC):
                for c in range(DC):
                    last = nc.tensor.matmul(i_bank[:, j:j + 1], mu_sq[:, c, j * P:(j + 1) * P], ones[:, 0:1],
                                            start=c == 0, stop=c == DC - 1)
            last.then_inc(mu_psum, 1)
            pe.wait_ge(mu_step, 4)
            nc.tensor.matmul(l_bank[0][:, 0:ES], ones[:, :], mu_diag[:, :, :], start=True, stop=True).then_inc(mu_psum, 1)
            transpose_x(0)
            pe.wait_ge(mu_ready, 1)
            batch_pairs_ahead(pe, batch)

        @block.scalar
        def _(act):
            def square(f, i):
                act.wait_ge(xa_ready, f + 1)
                for q in range(NC):
                    at_least(act, sumsq_ready, NC * f + q)
                    at_least(act, len_ready, f)
                    nc.scalar.activation(sq[:, :], xa[i][:, q, :], ACT.Square, accum_out=sumsq[:, q:q + 1]).then_inc(sumsq_ready, 1)

            def transposed_x(f, i):
                for c in range(DC):
                    act.wait_ge(xt_psum, DC * f + c + 1)
                    at_least(act, l_psum, 2 * (f - 1))
                    nc.scalar.copy(xT[i][0][:, c, :], x_bank[c][:, 0:N]).then_inc(xt_hi, 1)

            def exponentials(f, k):
                act.wait_ge(top_ready, 2 * f + k + 1)
                at_least(act, weight_ready, 4 * (f - 1) + 2 * k + 2)
                for r in range(2):
                    nc.scalar.activation(ex[k][:, r, :], l_bank[k][:, r * ES:(r + 1) * ES], ACT.Exp,
                                         bias=top[k][:, r:r + 1], accum_out=rsum[k][:, r:r + 1]).then_inc(ex_ready, 1)

            def round_x(f, i):
                at_least(act, i_psum, f - 1)
                act.wait_ge(xa_ready, f + 1)
                nc.scalar.copy(xaS[i][0][:, :, :], xa[i][:, :, :]).then_inc(xas_hi, 1)

            def batch(f, i, front, back, following, later, latest):
                g = f - 1
                if back:
                    act.wait_ge(t_psum, 2 * g + 1)
                    at_least(act, i_psum, g)
                    nc.scalar.copy(disp[0][:, :, :], t_bank[0][:, :].rearrange("p (q n) -> p q n", q=NC)).then_inc(disp_hi, 1)
                if front:
                    exponentials(f, 0)
                if back:
                    act.wait_ge(t_psum, 2 * g + 2)
                    nc.scalar.copy(st.comb[:, :, bass.ds(g, 1), :].rearrange("p j b n -> p (j b) n"),
                                   t_bank[1][:, :].rearrange("p (j n) -> p j n", j=EC)).then_inc(comb_stored, 1)
                if following:
                    transposed_x(f + 1, 1 - i)
                if later:
                    square(f + 2, i)
                if front:
                    exponentials(f, 1)
                if back:
                    act.wait_ge(i_psum, g + 1)
                    nc.scalar.copy(st.slots[:, :, bass.ds(g, 1), :].rearrange("p c b n -> p (c b) n"),
                                   i_bank[:, :].rearrange("p (c n) -> p c n", c=DC)).then_inc(slots_stored, 1)
                if following:
                    round_x(f + 1, 1 - i)

            square(0, 0)
            transposed_x(0, 0)
            square(1, 1)
            round_x(0, 0)
            batch_pairs_ahead(act, batch)

        @block.vector
        def _(dve):
            def unit(f, i):
                dve.wait_ge(lmin_ready, f + 1)
                at_least(dve, xu_ready, NC * f)
                nc.vector.reciprocal(inv_length[:, :], length_min[:, :]).then_inc(inv_ready, 1)
                dve.wait_ge(inv_ready, f + 1)
                at_least(dve, xt_psum, DC * f)
                for q in range(NC):
                    nc.vector.tensor_scalar(xu[:, q, :], xa[i][:, q, :], inv_length[:, q:q + 1], scale[:, 0:1],
                                            ALU.mult, ALU.mult).then_inc(xu_ready, 1)

            def transposed_x(f, i):
                for c in range(DC):
                    dve.wait_ge(xt_hi, DC * f + c + 1)
                    nc.vector.tensor_tensor(xT[i][1][:, c, :], x_bank[c][:, 0:N], fp32_of(xT[i][0][:, c, :]),
                                            ALU.subtract).then_inc(xt_lo, 1)

            def maxima(f, k):
                dve.wait_ge(l_psum, 2 * f + k + 1)
                nc.vector.tensor_reduce(top[k][:, :], l_bank[k][:, :].rearrange("p (r n) -> p r n", r=2), AX,
                                        ALU.max, negate=True).then_inc(top_ready, 1)

            def invert(f, k):
                dve.wait_ge(ex_ready, 4 * f + 2 * k + 2)
                nc.vector.reciprocal(rinv[k][:, :], rsum[k][:, :]).then_inc(rinv_ready, 1)

            def weigh(f, k):
                dve.wait_ge(rinv_ready, 2 * f + k + 1)
                at_least(dve, t_psum, 2 * (f - 1) + k + 1)
                for r in range(2):
                    nc.vector.tensor_scalar(weight[k][:, r, :], ex[k][:, r, :], rinv[k][:, r:r + 1], None,
                                            ALU.mult).then_inc(weight_ready, 1)

            def batch(f, i, front, back, following, later, latest):
                g = f - 1
                if later:
                    ln.normalise(dve, f + 2, xg_ready, 1)
                if following:
                    unit(f + 1, 1 - i)
                if front:
                    maxima(f, 0)
                if back:
                    dve.wait_ge(disp_hi, g + 1)
                    nc.vector.tensor_tensor(disp[1][:, :, :], t_bank[0][:, :].rearrange("p (q n) -> p q n", q=NC),
                                            fp32_of(disp[0][:, :, :]), ALU.subtract).then_inc(disp_lo, 1)
                if latest:
                    ln.statistics(dve, f + 3)
                if front:
                    invert(f, 0)
                    maxima(f, 1)
                    weigh(f, 0)
                if following:
                    transposed_x(f + 1, 1 - i)
                if front:
                    invert(f, 1)
                    weigh(f, 1)

            nc.vector.tensor_tensor(mu_sq[:, :, :], mu_raw[:, :, :], mu_raw[:, :, :], ALU.mult).then_inc(mu_step, 1)
            ln.statistics(dve, 0)
            dve.wait_ge(mu_psum, 1)
            nc.vector.tensor_copy(mu_sum[:, :], i_bank[:, 0:EC]).then_inc(mu_step, 1)
            ln.normalise(dve, 0, xg_ready, 1)
            ln.statistics(dve, 1)
            dve.wait_ge(mu_pow, 2)
            nc.vector.reciprocal(mu_inv[:, :], mu_max[:, :]).then_inc(mu_step, 1)
            dve.wait_ge(mu_step, 3)
            for j in range(EC):
                last = nc.vector.tensor_scalar(mu_diag[:, j, :], st.ident[:, :], mu_inv[:, j:j + 1], None, ALU.mult)
            last.then_inc(mu_step, 1)
            ln.normalise(dve, 1, xg_ready, 1)
            dve.wait_ge(mu_psum, 2)
            nc.vector.tensor_tensor(mu_unit[:, :, :], mu_raw[:, :, :], l_bank[0][:, 0:ES].unsqueeze(1).to_broadcast([P, DC, ES]),
                                    ALU.mult).then_inc(mu_step, 1)
            dve.wait_ge(mu_step, 5)
            nc.vector.tensor_copy(mu[0][:, :, :], mu_unit[:, :, :]).then_inc(mu_step, 1)
            dve.wait_ge(mu_step, 6)
            nc.vector.tensor_tensor(mu[1][:, :, :], mu_unit[:, :, :], fp32_of(mu[0][:, :, :]), ALU.subtract).then_inc(mu_ready, 1)
            dve.wait_ge(in_, 48)
            ln.statistics(dve, 2)
            unit(0, 0)
            transposed_x(0, 0)
            batch_pairs_ahead(dve, batch)

        @block.gpsimd
        def _(pool):
            poolt = Ticking(pool, m.sem("pool_ticks"))
            def affine(f, i):
                wait_apart(poolt, ln.ready, NC * f + NC)
                wait_apart(poolt, xa_ready, f)
                nc.gpsimd.tensor_tensor(xg[:, :, :], ln.xn[:, :, :], gamma[:, :].unsqueeze(1).to_broadcast([P, NC, D]),
                                        ALU.mult).then_inc(xg_ready, 1)
                wait_apart(poolt, xg_ready, f + 1)
                wait_apart(poolt, xu_ready, NC * (f - 1))
                wait_apart(poolt, xas_ready, f - 1)
                nc.gpsimd.tensor_tensor(xa[i][:, :, :], xg[:, :, :], beta[:, :].unsqueeze(1).to_broadcast([P, NC, D]),
                                        ALU.add).then_inc(xa_ready, 1)

            def lengths(f):
                wait_apart(poolt, sumsq_ready, NC * f + NC)
                wait_apart(poolt, lmin_ready, f)
                nc.gpsimd.tensor_tensor(length[:, :], sumsq[:, :], half[:, :], ALU.pow).then_inc(len_ready, 1)
                wait_apart(poolt, len_ready, f + 1)
                wait_apart(poolt, inv_ready, f)
                nc.gpsimd.tensor_scalar(length_min[:, :], length[:, :], NORM_EPS, None, ALU.max).then_inc(lmin_ready, 1)

            def split_x(f, i):
                wait_apart(poolt, xas_hi, f + 1)
                nc.gpsimd.tensor_tensor(xaS[i][1][:, :, :], xa[i][:, :, :], fp32_of(xaS[i][0][:, :, :]),
                                        ALU.subtract).then_inc(xas_ready, 1)

            def batch(f, i, front, back, following, later, latest):
                if front:
                    split_x(f, i)
                if later:
                    affine(f + 2, i)
                if latest:
                    ln.inverse_deviation(pool, f + 3)
                if later:
                    lengths(f + 2)

            pool.memset(ones[:, :], 1.0).then_inc(const_ready, 1)
            pool.memset(half[:, :], 0.5).then_inc(const_ready, 1)
            ln.inverse_deviation(pool, 0)
            wait_apart(poolt, mu_step, 2)
            wait_apart(poolt, const_ready, 2)
            nc.gpsimd.tensor_tensor(mu_norm[:, :], mu_sum[:, :], half[:, 0:EC], ALU.pow).then_inc(mu_pow, 1)
            wait_apart(poolt, mu_pow, 1)
            nc.gpsimd.tensor_scalar(mu_max[:, :], mu_norm[:, :], NORM_EPS, None, ALU.max).then_inc(mu_pow, 1)
            wait_apart(poolt, in_, 48)
            affine(0, 0)
            ln.inverse_deviation(pool, 1)
            lengths(0)
            affine(1, 1)
            lengths(1)
            ln.inverse_deviation(pool, 2)
            batch_pairs_ahead(pool, batch)


def experts(nc, d, st):
    with ExitStack() as stack:
        m = Memory(nc, stack, "exp")
        b_raw = m.sb("b_raw", [E, HID + D])
        b1, b2 = m.sb("b1", [HID, E]), m.sb("b2", [P, DC, E])
        w1_raw = [m.sb(f"w1_raw{i}", [P, DC, HID]) for i in range(2)]
        w2_raw = [m.sb(f"w2_raw{i}", [HID, D]) for i in range(2)]
        w1 = [m.split(f"w1_{i}", [P, DC, HID]) for i in range(2)]
        w2 = [m.split(f"w2_{i}", [HID, D]) for i in range(2)]
        xin = [m.split(f"xin{i}", [P, DC, B, S]) for i in range(2)]
        hid = [m.sb(f"hid{i}", [HID, B * S]) for i in range(2)]
        hT = [m.split(f"hT{i}", [HID, B * S]) for i in range(2)]
        b_bank = m.ps("b_bank")
        h_bank = [m.ps(f"h_bank{i}") for i in range(2)]
        o_bank = [m.ps(f"o_bank{i}") for i in range(2)]
        b_in, b_psum, b_ready = m.sem("b_in"), m.sem("b_psum"), m.sem("b_ready")
        w_in = [m.sem(f"w_in{i}") for i in range(2)]
        in_hi, in_lo, w2_hi, w2_lo = m.sem("in_hi"), m.sem("in_lo"), m.sem("w2_hi"), m.sem("w2_lo")
        h_psum, hid_ready, hid_hi, hid_lo = m.sem("h_psum"), m.sem("hid_ready"), m.sem("hid_hi"), m.sem("hid_lo")
        o_psum, out_stored = m.sem("o_psum"), m.sem("out_stored")
        stack.callback(m.end_phase)
        block = stack.enter_context(nc.Block())

        def slots_of(e):
            return st.slots[:, :, :, bass.ds(e * S, S)]

        @block.sync
        def _(sp):
            sp.dma_start(b_raw[:, 0:HID], d["L1_ffn_b1"]).then_inc(b_in, 16)
            sp.dma_start(b_raw[:, HID:], d["L1_ffn_b2"]).then_inc(b_in, 16)

            def load(e, i):
                sp.dma_start(w1_raw[i][:, :, :], d["L1_ffn_w1"][bass.ds(e, 1)].rearrange("a (c p) h -> p (a c) h", p=P)).then_inc(w_in[i], 16)
                sp.dma_start(w2_raw[i][:, :], d["L1_ffn_w2"][bass.ds(e, 1)].rearrange("a h n -> (a h) n")).then_inc(w_in[i], 16)

            for i in range(2):
                load(i, i)
            with sp.Fori(1, E // 2) as k:
                for i in range(2):
                    sp.wait_ge(w2_lo, 2 * k + i - 1)
                    load(2 * k + i, i)

        @block.tensor
        def _(pe):
            def up(e, i):
                pe.wait_ge(in_lo, e + 1)
                at_least(pe, hid_ready, e - 1)
                for n, (c, (a, b)) in enumerate((c, ab) for c in range(DC) for ab in PASSES):
                    last = nc.tensor.matmul(h_bank[i][0:HID, 0:B * S], w1[i][a][:, c, :], xin[i][b][:, c, :, :],
                                            start=n == 0, stop=n == 5)
                last.then_inc(h_psum, 1)

            def down(e, i):
                pe.wait_ge(hid_lo, e + 1)
                pe.wait_ge(w2_lo, e + 1)
                at_least(pe, out_stored, DC * (e - 1))
                for c in range(DC):
                    for n, (a, b) in enumerate(PASSES):
                        last = nc.tensor.matmul(o_bank[i][:, c * B * S:(c + 1) * B * S], w2[i][a][:, c * P:(c + 1) * P],
                                                hT[i][b][:, :], start=n == 0, stop=n == 2)
                last.then_inc(o_psum, 1)

            def step(e, i, front, back, following):
                if front:
                    up(e, i)
                if back:
                    down(e - 1, 1 - i)

            pe.wait_ge(b_in, 32)
            nc.tensor.transpose(b_bank[0:HID, 0:E], b_raw[:, 0:HID], st.ident[0:E, 0:E])
            for c in range(DC):
                last = nc.tensor.transpose(b_bank[:, (c + 1) * E:(c + 2) * E], b_raw[:, HID + c * P:HID + (c + 1) * P],
                                           st.ident[0:E, 0:E])
            last.then_inc(b_psum, 1)
            batch_pairs(pe, step)

        @block.scalar
        def _(act):
            def split_inputs(e, i):
                act.wait_ge(w_in[i], 32 * ((e - i) // 2 + 1) if isinstance(e, int) else 16 * (e - i) + 32)
                at_least(act, h_psum, e - 1)
                nc.scalar.copy(w1[i][0][:, :, :], w1_raw[i][:, :, :])
                nc.scalar.copy(xin[i][0][:, :, :, :], slots_of(e)).then_inc(in_hi, 1)

            def split_w2(e, i):
                at_least(act, o_psum, e - 1)
                nc.scalar.copy(w2[i][0][:, :], w2_raw[i][:, :]).then_inc(w2_hi, 1)

            def step(e, i, front, back, following):
                if following:
                    split_inputs(e + 1, 1 - i)
                if front:
                    act.wait_ge(h_psum, e + 1)
                    at_least(act, hid_lo, e - 1)
                    nc.scalar.activation(hid[i][:, :], h_bank[i][0:HID, 0:B * S], ACT.Gelu,
                                         bias=b1[:, bass.ds(e, 1)]).then_inc(hid_ready, 1)
                if following:
                    split_w2(e + 1, 1 - i)
                if back:
                    act.wait_ge(o_psum, e)
                    for c in range(DC):
                        act.wait_ge(in_lo, e)
                        out = st.slots[:, c, :, bass.ds((e - 1) * S, S)]
                        nc.scalar.activation(out, o_bank[1 - i][:, c * B * S:(c + 1) * B * S].rearrange("p (b s) -> p b s", b=B),
                                             ACT.Identity, bias=b2[:, c, bass.ds(e - 1, 1)]).then_inc(out_stored, 1)

            split_inputs(0, 0)
            split_w2(0, 0)
            act.wait_ge(b_ready, 2)
            batch_pairs(act, step)

        @block.vector
        def _(dve):
            def split_inputs(e, i):
                dve.wait_ge(in_hi, e + 1)
                nc.vector.tensor_tensor(w1[i][1][:, :, :], w1_raw[i][:, :, :], fp32_of(w1[i][0][:, :, :]), ALU.subtract)
                for c in range(DC):
                    last = nc.vector.tensor_tensor(xin[i][1][:, c, :, :], st.slots[:, c, :, bass.ds(e * S, S)],
                                                   fp32_of(xin[i][0][:, c, :, :]), ALU.subtract)
                last.then_inc(in_lo, 1)

            def split_w2(e, i):
                dve.wait_ge(w2_hi, e + 1)
                nc.vector.tensor_tensor(w2[i][1][:, :], w2_raw[i][:, :], fp32_of(w2[i][0][:, :]), ALU.subtract).then_inc(w2_lo, 1)

            def step(e, i, front, back, following):
                if following:
                    split_inputs(e + 1, 1 - i)
                if front:
                    dve.wait_ge(hid_ready, e + 1)
                    at_least(dve, o_psum, e - 1)
                    nc.vector.tensor_copy(hT[i][0][:, :], hid[i][:, :]).then_inc(hid_hi, 1)
                    dve.wait_ge(hid_hi, e + 1)
                    nc.vector.tensor_tensor(hT[i][1][:, :], hid[i][:, :], fp32_of(hT[i][0][:, :]), ALU.subtract).then_inc(hid_lo, 1)
                if following:
                    split_w2(e + 1, 1 - i)

            split_inputs(0, 0)
            split_w2(0, 0)
            dve.wait_ge(b_psum, 1)
            nc.vector.tensor_copy(b1[:, :], b_bank[0:HID, 0:E]).then_inc(b_ready, 1)
            nc.vector.tensor_copy(b2[:, :, :], b_bank[:, E:(DC + 1) * E].rearrange("p (c e) -> p c e", c=DC)).then_inc(b_ready, 1)
            batch_pairs(dve, step)


def combine(nc, d, st, out):
    with ExitStack() as stack:
        m = Memory(nc, stack, "comb")
        so = [m.sb(f"so{i}", [P, DC, ES]) for i in range(2)]
        soS = [m.split(f"soS{i}", [P, EC, D]) for i in range(2)]
        cT = [m.split(f"cT{i}", [P, EC, N]) for i in range(2)]
        y = [m.sb(f"y{i}", [P, NC, D]) for i in range(2)]
        s_bank = [m.ps(f"s_bank{i}") for i in range(2)]
        y_bank = [m.ps(f"y_bank{i}") for i in range(2)]
        so_ready, s_psum, so_hi, so_lo = m.sem("so_ready"), m.sem("s_psum"), m.sem("so_hi"), m.sem("so_lo")
        ct_hi, ct_lo, y_psum, y_ready = m.sem("ct_hi"), m.sem("ct_lo"), m.sem("y_psum"), m.sem("y_ready")
        y_out = [m.sem(f"y_out{i}") for i in range(2)]
        stack.callback(m.end_phase)
        block = stack.enter_context(nc.Block())

        @block.sync
        def _(sp):
            def store(f, i):
                sp.wait_ge(y_ready, f + 1)
                sp.dma_start(out[bass.ds(f, 1)].rearrange("b (q p) n -> p (b q) n", p=P), y[i][:, :, :]).then_inc(y_out[i], 16)

            with sp.Fori(0, B // 2) as k:
                for i in range(2):
                    store(2 * k + i, i)
            for i in range(2):
                sp.wait_ge(y_out[i], 16 * (B // 2))

        @block.tensor
        def _(pe):
            def step(f, i, front, back, following):
                g = f - 1
                if front:
                    pe.wait_ge(so_ready, f + 1)
                    at_least(pe, so_lo, f - 1)
                    for c in range(DC):
                        for j in range(EC):
                            last = nc.tensor.transpose(s_bank[i][:, j * D + c * P:j * D + (c + 1) * P],
                                                       so[i][:, c, j * P:(j + 1) * P], st.ident[:, :])
                    last.then_inc(s_psum, 1)
                if back:
                    pe.wait_ge(so_lo, g + 1)
                    pe.wait_ge(ct_lo, g + 1)
                    at_least(pe, y_ready, g - 1)
                    for q in range(NC):
                        for n, (j, (a, b)) in enumerate((j, ab) for j in range(EC) for ab in PASSES):
                            last = nc.tensor.matmul(y_bank[1 - i][:, q * D:(q + 1) * D], cT[1 - i][a][:, j, q * P:(q + 1) * P],
                                                    soS[1 - i][b][:, j, :], start=n == 0, stop=n == 5)
                    last.then_inc(y_psum, 1)

            batch_pairs(pe, step)

        @block.scalar
        def _(act):
            def step(f, i, front, back, following):
                if front:
                    at_least(act, y_psum, f - 1)
                    nc.scalar.copy(cT[i][0][:, :, :], st.comb[:, :, bass.ds(f, 1), :].rearrange("p j b n -> p (j b) n")).then_inc(ct_hi, 1)
                    act.wait_ge(s_psum, f + 1)
                    nc.scalar.copy(soS[i][0][:, :, :], s_bank[i][:, :].rearrange("p (j n) -> p j n", j=EC)).then_inc(so_hi, 1)

            batch_pairs(act, step)

        @block.vector
        def _(dve):
            def fetch(f, i):
                at_least(dve, s_psum, f - 1)
                nc.vector.tensor_copy(so[i][:, :, :], st.slots[:, :, bass.ds(f, 1), :].rearrange("p c b n -> p (c b) n")).then_inc(so_ready, 1)

            def step(f, i, front, back, following):
                g = f - 1
                if following:
                    fetch(f + 1, 1 - i)
                if front:
                    dve.wait_ge(so_hi, f + 1)
                    nc.vector.tensor_tensor(soS[i][1][:, :, :], s_bank[i][:, :].rearrange("p (j n) -> p j n", j=EC),
                                            fp32_of(soS[i][0][:, :, :]), ALU.subtract).then_inc(so_lo, 1)
                if back:
                    dve.wait_ge(y_psum, g + 1)
                    if isinstance(g, int):
                        at_least(dve, y_out[1 - i], 16 * (g // 2))
                    else:
                        dve.wait_ge(y_out[1 - i], 8 * (g - (1 - i)))
                    nc.vector.tensor_tensor(y[1 - i][:, :, :], y_bank[1 - i][:, :].rearrange("p (q n) -> p q n", q=NC),
                                            st.x[:, bass.ds(g, 1), :, :].rearrange("p b q n -> p (b q) n"), ALU.add).then_inc(y_ready, 1)

            fetch(0, 0)
            batch_pairs(dve, step)

        @block.gpsimd
        def _(pool):
            poolt = Ticking(pool, m.sem("pool_ticks"))
            def step(f, i, front, back, following):
                if front:
                    wait_apart(poolt, ct_hi, f + 1)
                    nc.gpsimd.tensor_tensor(cT[i][1][:, :, :], st.comb[:, :, bass.ds(f, 1), :].rearrange("p j b n -> p (j b) n"),
                                            fp32_of(cT[i][0][:, :, :]), ALU.subtract).then_inc(ct_lo, 1)

            batch_pairs(pool, step)


def moe(nc, d, st, out):
    with ExitStack() as stack:
        m = Memory(nc, stack, "moe")
        st.slots = m.sb("slots", [P, DC, B, ES])
        st.comb = m.sb("comb", [P, EC, B, N])
        route(nc, d, st)
        experts(nc, d, st)
        combine(nc, d, st, out)


class Store:
    pass


def build(nc, d, out, last_phase=5):
    with ExitStack() as stack:
        m = Memory(nc, stack, "all")
        st = Store()
        st.x = m.sb("x", [P, B, NC, D])
        st.raw = m.sb("raw", [P, 4096])
        st.ident = m.sb("ident", [P, P])
        st.minus_half = m.sb("minus_half", [P, NC])
        st.head_mask0 = m.sb("head_mask0", [P, 2])
        st.head_mask1 = m.sb("head_mask1", [P, 8])
        with ExitStack() as kv_stack:
            kv = Memory(nc, kv_stack, "kv")
            st.key0 = kv.sb("key0", [P, B, SK])
            st.key1 = kv.sb("key1", [P, DC, B, SK])
            st.val0 = kv.sb("val0", [P, B, DK0])
            st.val1 = kv.sb("val1", [P, B, D])
            prologue(nc, d, st)
            if last_phase >= 1:
                attention(nc, d, st, 0)
            if last_phase >= 2:
                ffn(nc, d, st)
            if last_phase >= 3:
                attention(nc, d, st, 1)
        if last_phase >= 4:
            moe(nc, d, st, out)
        else:
            o_out = m.sem("o_out")
            block = stack.enter_context(nc.Block())

            @block.sync
            def _(sp):
                for b in range(B):
                    sp.dma_start(out[b].rearrange("(q p) e -> p q e", p=P), st.x[:, b, :, :]).then_inc(o_out, 16)
                sp.wait_ge(o_out, 16 * B)


def constants():
    p = np.arange(P)
    positions = np.zeros((P, N), np.float32)
    positions[0:3], positions[3:6] = np.arange(N), 1.0
    causal = np.where(p[:, None] >= np.arange(SK)[None, :], 0.0, -1e9).astype(np.float32)
    return {
        "ident": np.eye(P, dtype=np.float32),
        "head_mask0": (p[:, None] // DK0 == np.arange(P // DK0)).astype(np.float32),
        "head_mask1": (p[:, None] // DK1 == np.arange(P // DK1)).astype(np.float32),
        "causal": np.concatenate([causal, causal], 1),
        "positions": positions,
        "neg_k": np.broadcast_to(-np.arange(SK, dtype=np.float32), (H, SK)).copy(),
    }


def kernel(**inputs):
    import concourse.bacc as bacc
    from concourse.bass_utils import run_bass_kernel_spmd

    nc = bacc.Bacc("TRN2", target_bir_lowering=False, num_devices=1)
    arrays, d = {}, {}
    for name, a in {**inputs, **constants()}.items():
        a = np.ascontiguousarray(a)
        arrays[f"in_{name}"] = a
        d["ctx" if name == "ctx_1024" else name] = nc.dram_tensor(
            f"in_{name}", a.shape, mybir.dt.from_np(a.dtype), kind="ExternalInput").ap()
    out = nc.dram_tensor("out", (B, N, D), F32, kind="ExternalOutput").ap()
    build(nc, d, out)
    r = run_bass_kernel_spmd(nc, [arrays], core_ids=[0])
    return r.results[0]["out"]
```
